# Optimizing a Trainium2 kernel written in Bass

```python
import numpy as np
import jax
import jax.numpy as jnp

def _softmax(x, axis=-1):
    return jax.nn.softmax(x, axis=axis)

def _gelu(x):
    return jax.nn.gelu(x, approximate=True)

def _silu(x):
    return jax.nn.silu(x)

def _sigmoid(x):
    return jax.nn.sigmoid(x)

def _layernorm(x, axis=-1, eps=1e-05):
    m = jnp.mean(x, axis=axis, keepdims=True)
    v = jnp.var(x, axis=axis, keepdims=True)
    return (x - m) / jnp.sqrt(v + eps)

def _scatter_add(tgt, idx, src, axis=0):
    return tgt.at[idx].add(src)

def _segment_sum(src, seg, n):
    return jax.ops.segment_sum(src, seg, n)
kernel_name = 'mk_seq_preln_d1_jaxref_r8_f2b9a6'

def setup_inputs(seed: int=0):
    np.random.seed(seed)
    _w = jnp.asarray

    def _L0_attn_setup():
        import jax, jax.numpy as jnp
        import numpy as np
        D_MODEL = 256
        N_HEADS = 16
        N_KV = 4
        GROUP = N_HEADS // N_KV
        D_K = D_MODEL // N_HEADS
        D_V = D_MODEL // N_KV
        THETA = 10000.0
        Q_DIM = N_HEADS * D_K
        K_DIM = N_KV * D_K
        V_DIM = N_KV * D_V

        def _apply_rope(t, sin, cos):
            half = t.shape[-1] // 2
            x1, x2 = (t[..., :half], t[..., half:])
            rot = jnp.concatenate([-x2, x1], axis=-1)
            return t * cos + rot * sin
        key = jax.random.key(seed)
        k1, k2, k3 = jax.random.split(key, 3)
        x = jax.random.normal(k1, (2, 256, D_MODEL), dtype=jnp.float32)
        W_attn = jax.random.normal(k2, (D_MODEL, Q_DIM + K_DIM + V_DIM), dtype=jnp.float32) * 0.02
        W_out = jax.random.normal(k3, (N_HEADS * D_V, D_MODEL), dtype=jnp.float32) * 0.02
        b_out = jnp.zeros((D_MODEL,), dtype=jnp.float32)
        return {'x': x, 'W_attn': W_attn, 'W_out': W_out, 'b_out': b_out}
    _L0_attn_in = _L0_attn_setup()

    def _L0_ffn_setup():
        import jax, jax.numpy as jnp
        import numpy as np
        EPS = 1e-08

        def _quantize(w):
            gamma = jnp.mean(jnp.abs(w))
            return jnp.clip(jnp.round(w / (gamma + EPS)), -1.0, 1.0)

        def _bitlinear(x, w):
            return jnp.matmul(x, _quantize(w).T)
        key = jax.random.key(seed)
        k1, k2, k3, k4 = jax.random.split(key, 4)
        d, h = (256, 704)
        x = jax.random.normal(k1, (4, 256, d), dtype=jnp.float32)
        w1 = jax.random.normal(k2, (h, d), dtype=jnp.float32)
        w2 = jax.random.normal(k3, (h, d), dtype=jnp.float32)
        w3 = jax.random.normal(k4, (d, h), dtype=jnp.float32)
        return {'x': x, 'w1': w1, 'w2': w2, 'w3': w3}
    _L0_ffn_in = _L0_ffn_setup()
    _d = {'L0_attn_x': _L0_attn_in['x'], 'L0_attn_W_attn': _L0_attn_in['W_attn'], 'L0_attn_W_out': _L0_attn_in['W_out'], 'L0_attn_b_out': _L0_attn_in['b_out'], 'L0_ffn_w1': _L0_ffn_in['w1'], 'L0_ffn_w2': _L0_ffn_in['w2'], 'L0_ffn_w3': _L0_ffn_in['w3']}
    _x0 = _d['L0_attn_x']
    _d['L0_attn_x'] = jax.random.normal(jax.random.fold_in(jax.random.key(seed), 1), (1, 2048, 256), dtype=_x0.dtype)
    del _x0
    return _d

def reference(L0_attn_x, L0_attn_W_attn, L0_attn_W_out, L0_attn_b_out, L0_ffn_w1, L0_ffn_w2, L0_ffn_w3):

    def _L0_attn_ref(x, W_attn, W_out, b_out):
        import jax, jax.numpy as jnp
        import numpy as np
        D_MODEL = 256
        N_HEADS = 16
        N_KV = 4
        GROUP = N_HEADS // N_KV
        D_K = D_MODEL // N_HEADS
        D_V = D_MODEL // N_KV
        THETA = 10000.0
        Q_DIM = N_HEADS * D_K
        K_DIM = N_KV * D_K
        V_DIM = N_KV * D_V

        def _apply_rope(t, sin, cos):
            half = t.shape[-1] // 2
            x1, x2 = (t[..., :half], t[..., half:])
            rot = jnp.concatenate([-x2, x1], axis=-1)
            return t * cos + rot * sin
        B, L, _ = x.shape
        qkv = x @ W_attn
        q = qkv[..., :Q_DIM].reshape(B, L, N_HEADS, D_K).transpose(0, 2, 1, 3)
        k = qkv[..., Q_DIM:Q_DIM + K_DIM].reshape(B, L, N_KV, D_K).transpose(0, 2, 1, 3)
        v = qkv[..., Q_DIM + K_DIM:].reshape(B, L, N_KV, D_V).transpose(0, 2, 1, 3)
        inv_freq = 1.0 / THETA ** (jnp.arange(0, D_K, 2, dtype=jnp.float32) / D_K)
        freqs = jnp.arange(L, dtype=jnp.float32)[:, None] * inv_freq[None, :]
        ang = jnp.concatenate([freqs, freqs], axis=-1)
        sin, cos = (jnp.sin(ang), jnp.cos(ang))
        q = _apply_rope(q.astype(jnp.float32), sin, cos).astype(x.dtype)
        k = _apply_rope(k.astype(jnp.float32), sin, cos).astype(x.dtype)
        qg = q.reshape(B, N_KV, GROUP, L, D_K)
        scores = jnp.einsum('bkgqd,bkld->bkgql', qg, k) / D_K ** 0.5
        probs = jax.nn.softmax(scores, axis=-1)
        ctx = jnp.einsum('bkgql,bkle->bkgqe', probs, v)
        ctx = ctx.reshape(B, N_HEADS, L, D_V).transpose(0, 2, 1, 3).reshape(B, L, N_HEADS * D_V)
        return ctx @ W_out + b_out

    def _L0_ffn_ref(x, w1, w2, w3):
        import jax, jax.numpy as jnp
        import numpy as np
        EPS = 1e-08

        def _quantize(w):
            gamma = jnp.mean(jnp.abs(w))
            return jnp.clip(jnp.round(w / (gamma + EPS)), -1.0, 1.0)

        def _bitlinear(x, w):
            return jnp.matmul(x, _quantize(w).T)
        x1 = _bitlinear(x, w1)
        x2 = _bitlinear(x, w2)
        hidden = jax.nn.sigmoid(x1) * x2
        return _bitlinear(hidden, w3)
    x = L0_attn_x
    x = x + _L0_attn_ref(_layernorm(x, axis=-1), L0_attn_W_attn, L0_attn_W_out, L0_attn_b_out)
    x = x + _L0_ffn_ref(_layernorm(x, axis=-1), L0_ffn_w1, L0_ffn_w2, L0_ffn_w3)
    return x

_drawn_inputs = setup_inputs


def setup_inputs(seed=0):
    import zlib

    import numpy as np

    out = dict(_drawn_inputs(seed))
    spreads = {'L0_attn_b_out': (0.0, 0.304)}
    factors = {'L0_attn_W_attn': 6.77, 'L0_attn_W_out': 7.555}
    for name, (base, spread) in spreads.items():
        noise = np.random.default_rng([zlib.crc32(name.encode()), seed]).standard_normal(out[name].shape)
        drawn = base * np.exp(spread * noise) if base else spread * noise
        out[name] = jnp.asarray(drawn.astype(out[name].dtype))
    for name, factor in factors.items():
        out[name] = (out[name] * factor).astype(out[name].dtype)
    return out
```

```python
import concourse.bass as bass
from concourse import mybir
from contextlib import ExitStack
import numpy as np

fp32 = mybir.dt.float32
bf16 = mybir.dt.bfloat16
fp16 = mybir.dt.float16
u32 = mybir.dt.uint32
ALU = mybir.AluOpType
ACT = mybir.ActivationFunctionType
AX = mybir.AxisListType

L, D = 2048, 256
NH, NKV, DK, DV = 16, 4, 16, 64
HF = DK // 2
FF = 704
P = 128
NT = L // P
NC = L // 512
DC = D // P
NB = NH * NC
STEPS = NT // 2
KROWS = 6 * DK
MROW = KROWS
QROWS = KROWS + 4
SHIFT = 8.3125
VW = 130
POOLW = 640
FCH = [(i * P, min(P, FF - i * P)) for i in range((FF + P - 1) // P)]
OC = NH * DV // P
LN_VAR = 2 * NT + 1
DCH_BEFORE_END = LN_VAR + 5 + 9 * NC + 5
LN2_VAR = DCH_BEFORE_END + 3 * NT + 1
PRW = 129
TERMS = [(0, 0), (0, 1), (1, 0), (1, 1), (0, 2), (2, 0)]


def layer(nc, x, w_qkv, w_out, b_out, w1t, w2t, w3t, cos_t, sin_t, ident, out):
    q_parts = nc.dram_tensor("q_parts", (3, 2, P, L), bf16, kind="Internal").ap()
    k_parts = nc.dram_tensor("k_parts", (3, 2, NKV * HF, L), bf16, kind="Internal").ap()

    ctx = ExitStack()
    with ctx:
        def sb(name, shape, dt):
            return ctx.enter_context(nc.sbuf_tensor(name, shape, dt))

        def sem(name):
            return ctx.enter_context(nc.semaphore(name))

        QC = sb("QC", [P, NB, 512], bf16)
        KA = sb("KA", [P, NKV * L], bf16)
        VP = sb("VP", [P, NT, NKV, VW], fp16)
        PF = sb("PF", [P, 4, 1024], fp32)
        PR = sb("PR", [P, 4, 1024], fp16)
        MX = sb("MX", [P, 4, 4], fp32)
        NM = sb("NM", [P, 4], fp32)
        R1 = sb("R1", [P, 4], fp32)
        MP = sb("MP", [P, 4, 4], bf16)
        EV = sb("EV", [P, 4, 129], fp32)
        CS = sb("CS", [P, 4, DV], fp32)
        RR = sb("RR", [P, 4], fp32)
        XS = sb("XS", [P, NT, D], fp32)
        WO = sb("WO", [P, OC, D], fp32)
        W1Q = sb("W1Q", [P, DC, FF], fp16)
        W2Q = sb("W2Q", [P, DC, FF], fp16)
        W3Q = sb("W3Q", [P, len(FCH), D], fp16)
        RW1 = sb("RW1", [P, DC * FF], fp32)
        RW2 = sb("RW2", [P, DC * FF], fp32)
        RW3 = sb("RW3", [P, len(FCH) * D], fp32)
        PT = sb("PT", [P, 2, 3, 3, 512], bf16)
        ID = sb("ID", [P, P], fp32)
        IDB = sb("IDB", [P, P], bf16)
        ONES = sb("ONES", [P, P], fp32)
        BO = sb("BO", [P, D], fp32)
        ST = sb("ST", [P, NT, 6], fp32)
        MV = sb("MV", [P, NT, 2], fp32)
        RS = sb("RS", [P, 6, NT], fp32)
        WS = sb("WS", [P, 16], fp32)
        SC = sb("SC", [P, 8], fp32)

        QCF = QC[:, :, :].rearrange("p b n -> p (b n)").bitcast(fp32)
        XN = QCF[:, 0:4096].rearrange("p (t n) -> p t n", t=NT)
        XNT = QCF[:, 4096:8192].rearrange("p (c t) -> p c t", c=DC)
        COS = QCF[:, 8192:10240]
        SIN = QCF[:, 10240:12288]
        RT = QCF[:, 12288:16384].rearrange("p (s n) -> p s n", n=512)
        WQ = PR[:, :, :].rearrange("p a b -> p (a b)").bitcast(fp32)[:, 0:1152].rearrange("p (c n) -> p c n", c=DC)
        VF = PF[:, :, :].rearrange("p a b -> p (a b)")
        QF = QC[:, :, :].rearrange("p b n -> p (b n)").bitcast(fp32).rearrange("p (b i e) -> p b i e", b=NB, i=4)
        CT = KA[:, :].bitcast(fp32).rearrange("p (r i c t) -> p r i c t", r=2, i=2, c=OC)
        X2 = PF[:, :, :].rearrange("p a b -> p (a b)").rearrange("p (t n) -> p t n", t=NT)
        T2H = PR[:, :, :].rearrange("p a b -> p (a b)").rearrange("p (c t) -> p c t", c=DC)
        T2L = KA[:, 4096:8192].bitcast(fp16).rearrange("p (c t) -> p c t", c=DC)
        HP = QCF[:, 0:6144].bitcast(fp16).rearrange("p (r q f t) -> p r q f t", r=2, q=2, f=len(FCH))
        SG = QCF[:, 8192:9216].rearrange("p (r t) -> p r t", r=2)
        HD = QCF[:, 9216:11264].rearrange("p (r t) -> p r t", r=4)
        PHI = PF[:, :, :].rearrange("p a b -> p (a b)").bitcast(bf16)\
            .rearrange("p (a b two) -> p a b two", a=4, two=2)[:, :, :, 1]
        KAT = KA[:, :]

        PS = ctx.enter_context(nc.psum_tensor("PS", [P, 8, 512], fp32))
        SCO = PS[:, 0:4, :]
        ACC = PS[:, 6:8, :].rearrange("p b (i n) -> p (b i) n", i=2)
        MT = PS[:, 4, :].bitcast(bf16)

        xin = [sem(f"xin{j}") for j in range(NC)]
        (wq_in, tab_in, id_in, bo_in, wo_in) = map(sem, ("wq_in", "tab_in", "id_in", "bo_in", "wo_in"))
        rw_in = [sem(f"rw_in{i}") for i in range(3)]
        (ones_set, idb_set, cst_set) = map(sem, ("ones_set", "idb_set", "cst_set"))
        dch = sem("dch")
        (std_a, xn_ready, tr_ready, xnt_a, xnt_d) = map(sem, ("std_a", "xn_ready", "tr_ready", "xnt_a", "xnt_d"))
        (k_ready, q_ready, v_ready, v_sb, roped, hi_a, rem_d, mid_a, low_d) = map(sem, (
            "k_ready", "q_ready", "v_ready", "v_sb", "roped", "hi_a", "rem_d", "mid_a", "low_d"))
        parts_out = [sem(f"parts_out{i}") for i in range(2)]
        (ops_in, k_ones, amax_d, aall_p, vscale, v_hi, vp_ready) = map(sem, (
            "ops_in", "k_ones", "amax_d", "aall_p", "vscale", "v_hi", "vp_ready"))
        (wabs, wsum, wgam, pch) = map(sem, ("wabs", "wsum", "wgam", "pch"))
        s_ready = sem("s_ready")
        e_done = sem("e_done")
        x_ready = sem("x_ready")
        x_read = sem("x_read")
        nm_d = sem("nm_d")
        mt_ready = sem("mt_ready")
        m_rows = sem("m_rows")
        r_pool = sem("r_pool")
        r_dve = sem("r_dve")
        pv_done = sem("pv_done")
        evac = sem("evac")
        norm_d = sem("norm_d")
        (ct_ready, ct_a, ct_d, y_ready, y_read, t2_ready, t2_hi, t2_lo) = map(sem, (
            "ct_ready", "ct_a", "ct_d", "y_ready", "y_read", "t2_ready", "t2_hi", "t2_lo"))
        (x2_ready, std2_a, g_ready, sig_a, hid_d, hh_a, hl_d, o_ready, o_sb, o_out) = map(sem, (
            "x2_ready", "std2_a", "g_ready", "sig_a", "hid_d", "hh_a", "hl_d", "o_ready", "o_sb", "o_out"))
        block = ctx.enter_context(nc.Block())

        def kv_of(b):
            return b // (NB // NKV)

        def max_tiles(s):
            return [(1 if s < 2 else 2, (2 * s + 12) % 16 + n) for n in range(2)]

        def context_half(eng, copy, done, m, i, hp):
            eng.wait_ge(ct_ready, m + 1)
            if m >= 2 and hp == 0:
                eng.wait_ge(y_ready, 2 * (m - 1))
            copy(CT[64 * hp:64 * hp + 64, m % 2, i, :, :].rearrange("p (b c) t -> p b (c t)", b=2),
                 PS[64 * i:64 * i + 64, 2 * hp:2 * hp + 2, :]).then_inc(done, 1)

        @block.sync
        def _(sp):
            sp.dma_start(ID[:], ident).then_inc(id_in, 16)
            for j in range(NC):
                sp.dma_start(XS[:, 4 * j:4 * j + 4, :],
                             x[j * 512:(j + 1) * 512, :].rearrange("(t p) d -> p t d", p=P)).then_inc(xin[j], 16)
            sp.dma_start(WQ, w_qkv.rearrange("(c p) n -> p c n", p=P)).then_inc(wq_in, 16)
            sp.dma_start(COS, cos_t).then_inc(tab_in, 16)
            sp.dma_start(SIN, sin_t).then_inc(tab_in, 16)
            sp.dma_start(RW1[:, :].rearrange("p (c n) -> p c n", c=DC),
                         w1t.rearrange("(c p) n -> p c n", p=P)).then_inc(rw_in[0], 16)
            sp.dma_start(RW2[:, :].rearrange("p (c n) -> p c n", c=DC),
                         w2t.rearrange("(c p) n -> p c n", p=P)).then_inc(rw_in[1], 16)
            nf = FF // P
            sp.dma_start(RW3[:, 0:nf * D].rearrange("p (c n) -> p c n", c=nf),
                         w3t[0:nf * P, :].rearrange("(c p) n -> p c n", p=P)).then_inc(rw_in[2], 16)
            sp.dma_start(RW3[0:FF - nf * P, nf * D:], w3t[nf * P:, :]).then_inc(rw_in[2], 16)
            sp.dma_start(BO[:], b_out.partition_broadcast(P)).then_inc(bo_in, 16)
            sp.dma_start(WO[:, :, :], w_out.rearrange("(c p) n -> p c n", p=P)).then_inc(wo_in, 16)
            for i in range(3 * NC):
                j, t = divmod(i, 3)
                tok = slice(j * 512, (j + 1) * 512)
                sp.wait_ge(low_d, i + 1)
                if t == 0:
                    for h in range(2):
                        sp.dma_start(k_parts[:, h, :, tok].rearrange("q r n -> r q n"),
                                     PT[32 * h:32 * h + 32, j % 2, 0, :, :]).then_inc(parts_out[j % 2], 16)
                else:
                    sp.dma_start(q_parts[:, t - 1, :, tok].rearrange("q r n -> r q n"),
                                 PT[:, j % 2, t, :, :]).then_inc(parts_out[j % 2], 16)
            sp.wait_ge(parts_out[0], 128)
            sp.wait_ge(parts_out[1], 128)
            for g, (qp, kp) in enumerate(TERMS):
                for h in range(2):
                    r = 2 * HF * g + HF * h
                    sp.dma_start(KA[r:r + HF, :].rearrange("f (k t) -> f k t", k=NKV),
                                 k_parts[kp, h, :, :].rearrange("(k f) t -> f k t", f=HF)).then_inc(ops_in, 16)
                    sp.dma_start(QC[r:r + HF, :, :].rearrange("f (a b) n -> f a (b n)", a=NH),
                                 q_parts[qp, h, :, :].rearrange("(a f) t -> f a t", f=HF)).then_inc(ops_in, 16)
            for n in range(NT):
                sp.wait_ge(o_sb, n + 1)
                sp.dma_start(out[n * P:(n + 1) * P, :], XS[:, n, :]).then_inc(o_out, 16)
            sp.wait_ge(o_out, 16 * NT)

        @block.gpsimd
        def _(pool):
            nc.gpsimd.memset(RW3[64:128, (FF // P) * D:], 0.0).then_inc(pch, 1)
            pool.wait_ge(pch, 1)
            nc.gpsimd.memset(KA[MROW:MROW + 4, :], 1.0).then_inc(k_ones, 1)
            pool.wait_ge(k_ones, 1)
            nc.gpsimd.memset(ONES[:], 1.0).then_inc(ones_set, 1)
            nc.gpsimd.memset(VP[:, :, :, DV:DV + 1], 1.0).then_inc(cst_set, 1)
            nc.gpsimd.memset(MP[:, :, 3:4], SHIFT).then_inc(cst_set, 1)
            pool.wait_ge(amax_d, 1)
            nc.gpsimd.partition_all_reduce(SC[:, 1:2], SC[:, 0:1], P, bass.bass_isa.ReduceOp.max).then_inc(aall_p, 1)
            pool.wait_ge(wgam, 1)
            done = 1
            for i, (raw, q) in enumerate(((RW1, W1Q), (RW2, W2Q), (RW3, W3Q))):
                g = WS[:, 12 + i:13 + i]
                nc.gpsimd.tensor_scalar(raw[:, :], raw[:, :], g, -1.0, ALU.mult, ALU.max).then_inc(pch, 1)
                done += 1
                pool.wait_ge(pch, done)
                nc.gpsimd.tensor_scalar(raw[:, :], raw[:, :], 1.0, 12582912.0, ALU.min, ALU.add).then_inc(pch, 1)
                done += 1
                pool.wait_ge(pch, done)
                nc.gpsimd.tensor_scalar(q[:, :, :].rearrange("p c n -> p (c n)"), raw[:, :], -12582912.0, None,
                                        ALU.add).then_inc(pch, 1)
                done += 1
            pool.wait_ge(pch, done)

            def pool_block(b, first=False):
                for s in range(STEPS):
                    t = 8 * b + s
                    pool.wait_ge(e_done, t + 1)
                    if not (first and s < 4):
                        pool.wait_ge(pv_done, t - 3)
                    nc.gpsimd.tensor_tensor(PR[:, s % 4, 0:POOLW], PF[:, s % 4, 0:POOLW], PHI[:, s % 4, 0:POOLW],
                                            ALU.subtract).then_inc(r_pool, 1)

            pool_block(0, first=True)
            with pool.Fori(1, NB - 2) as b:
                pool_block(b)
            pool_block(NB - 2)
            pool_block(NB - 1)

        @block.scalar
        def _(act):
            act.wait_ge(dch, LN_VAR)
            nc.scalar.activation(RS[:, 1, :], RS[:, 0, :], ACT.Sqrt).then_inc(std_a, 1)
            for j in range(NC):
                act.wait_ge(tr_ready, j + 1)
                nc.scalar.copy(XNT[:, 0, j * 512:(j + 1) * 512], PS[:, 2 * j, :]).then_inc(xnt_a, 1)
            w_abs = (W1Q, W2Q, W3Q)
            for i, raw in enumerate((RW1, RW2, RW3)):
                act.wait_ge(rw_in[i], 16 if i < 2 else 32)
                if i == 2:
                    act.wait_ge(pch, 1)
                nc.scalar.activation(w_abs[i][:, :, :].rearrange("p c n -> p (c n)").bitcast(bf16), raw[:, :], ACT.Abs, accum_out=WS[:, i:i + 1]).then_inc(wabs, 1)
            def hi(i):
                j, t = divmod(i, 3)
                rows = 64 if t == 0 else P
                act.wait_ge(roped, i + 1)
                if i >= 6:
                    act.wait_ge(parts_out[j % 2], 64 * (j // 2))
                nc.scalar.copy(PT[0:rows, j % 2, t, 0, :], RT[0:rows, 2 + i % 3, :]).then_inc(hi_a, 1)

            def mid(i):
                j, t = divmod(i, 3)
                rows = 64 if t == 0 else P
                act.wait_ge(rem_d, i + 1)
                nc.scalar.copy(PT[0:rows, j % 2, t, 1, :], RT[0:rows, 5 + i % 3, :]).then_inc(mid_a, 1)

            for i in range(3 * NC + 1):
                if i < 3 * NC:
                    hi(i)
                if i >= 1:
                    mid(i - 1)
                if i < 3 * NC and i % 3 == 1:
                    for n in (2 * (i // 3), 2 * (i // 3) + 1):
                        act.wait_ge(v_ready, n + 1)
                        nc.scalar.copy(VF[:, n * 512:(n + 1) * 512], PS[:, 6 + n % 2, :]).then_inc(v_sb, 1)
            act.wait_ge(vscale, 1)
            nc.scalar.activation(VP[:, :, :, 0:DV].rearrange("p t k e -> p (t k) e"),
                                 VF.rearrange("p (a e) -> p a e", e=DV), ACT.Copy, scale=SC[:, 5:6]).then_inc(v_hi, 1)

            def take_out(b):
                act.wait_ge(pv_done, 8 * b + 8)
                nc.scalar.copy(EV[:, :, :], ACC[:, :, 0:129]).then_inc(evac, 1)

            def act_block(b, first=False):
                for s in range(STEPS):
                    t = 8 * b + s
                    act.wait_ge(s_ready, t + 1)
                    if not (first and s < 4):
                        act.wait_ge(pv_done, t - 3)
                    nc.scalar.activation(PF[:, s % 4, :].rearrange("p (k n) -> p k n", k=2),
                                         SCO[:, 2 * (s % 2):2 * (s % 2) + 2, :], ACT.Exp).then_inc(e_done, 1)
                    if s == 1 and not first:
                        take_out(b - 1)

            act.wait_ge(vp_ready, 1)
            act_block(0, first=True)
            with act.Fori(1, NB - 2) as b:
                act_block(b)
            act_block(NB - 2)
            act_block(NB - 1)
            take_out(NB - 1)

            for n in range(2 * (NT // 2)):
                context_half(act, nc.scalar.copy, ct_a, n // 2, 0, n % 2)
            act.wait_ge(dch, LN2_VAR)
            nc.scalar.activation(RS[:, 1, :], RS[:, 0, :], ACT.Sqrt).then_inc(std2_a, 1)
            for i in range(2 * NC):
                act.wait_ge(t2_ready, i + 1)
                nc.scalar.copy(T2H[:, i % 2, (i // 2) * 512:(i // 2) * 512 + 512], PS[:, i, :]).then_inc(t2_hi, 1)
            def hidden_hi(i):
                j, f = divmod(i, len(FCH))
                act.wait_ge(hid_d, i + 1)
                if j >= 2:
                    act.wait_ge(o_ready, 4 * (j - 1))
                rows = FCH[f][1]
                nc.scalar.copy(HP[0:rows, j % 2, 0, f, :], HD[0:rows, i % 4, :]).then_inc(hh_a, 1)

            NG = NC * len(FCH)
            for i in range(NG + 1):
                if i < NG:
                    rows = FCH[i % len(FCH)][1]
                    act.wait_ge(g_ready, i + 1)
                    if i >= 2:
                        act.wait_ge(hid_d, i - 1)
                    nc.scalar.activation(SG[0:rows, i % 2, :], PS[0:rows, 2 * (i % 3), :],
                                         ACT.Sigmoid).then_inc(sig_a, 1)
                if i >= 1:
                    hidden_hi(i - 1)

        @block.vector
        def _(dve):
            count = [0]

            def step(ins):
                ins.then_inc(dch, 1)
                count[0] += 1
                return count[0]

            def need(n):
                dve.wait_ge(dch, n)

            def rstd(std, mark):
                n = step(nc.vector.tensor_scalar(RS[:, 0, :], MV[:, :, 1], 1e-5, None, ALU.add))
                assert n == mark, n
                dve.wait_ge(std, 1)
                need(step(nc.vector.reciprocal(RS[:, 2, :], RS[:, 1, :])))
                need(step(nc.vector.tensor_tensor(RS[:, 3, :], RS[:, 2, :], RS[:, 2, :], ALU.mult)))
                need(step(nc.vector.tensor_tensor(RS[:, 4, :], RS[:, 3, :], RS[:, 0, :], ALU.mult)))
                need(step(nc.vector.tensor_scalar(RS[:, 3, :], RS[:, 4, :], -0.5, 1.5, ALU.mult, ALU.add)))
                need(step(nc.vector.tensor_tensor(RS[:, 5, :], RS[:, 2, :], RS[:, 3, :], ALU.mult)))

            for n in range(NT):
                if n % 4 == 0:
                    dve.wait_ge(xin[n // 4], 16)
                last = step(nc.vector.bn_stats(ST[:, n, :], XS[:, n, :]))
                if n >= 1:
                    need(last - 1 if n == 1 else last - 2)
                    step(nc.vector.bn_aggr(MV[:, n - 1, :], ST[:, n - 1, :]))
            need(count[0] - 1)
            need(step(nc.vector.bn_aggr(MV[:, NT - 1, :], ST[:, NT - 1, :])))
            rstd(std_a, LN_VAR)
            for n in range(NT):
                nc.vector.tensor_scalar(XN[:, n, :], XS[:, n, :], MV[:, n, 0:1], RS[:, 5, n:n + 1],
                                        ALU.subtract, ALU.mult).then_inc(xn_ready, 1)
            dve.wait_ge(id_in, 16)
            nc.vector.tensor_copy(IDB[:], ID[:]).then_inc(idb_set, 1)
            for j in range(NC):
                dve.wait_ge(tr_ready, j + 1)
                nc.vector.tensor_copy(XNT[:, 1, j * 512:(j + 1) * 512], PS[:, 2 * j + 1, :]).then_inc(xnt_d, 1)

            def rope(i):
                j, t = divmod(i, 3)
                tok = slice(j * 512, (j + 1) * 512)
                if i >= 3:
                    dve.wait_ge(hi_a, i - 2)
                    dve.wait_ge(rem_d, i - 2)
                if t == 0:
                    dve.wait_ge(k_ready, j + 1)
                    kp = PS[:, 4 + j % 2, :]
                    n = []
                    for o, a, tab in ((0, 0, COS), (32, 32, COS)):
                        n.append(step(nc.vector.tensor_tensor(RT[o:o + 32, 0, :], kp[a:a + 32, :],
                                                              tab[a:a + 32, tok], ALU.mult)))
                    for o, a, tab in ((0, 32, SIN), (32, 0, SIN)):
                        n.append(step(nc.vector.tensor_tensor(RT[o:o + 32, 1, :], kp[a:a + 32, :],
                                                              tab[a:a + 32, tok], ALU.mult)))
                    need(n[-1])
                    step(nc.vector.tensor_tensor(RT[0:32, 2 + i % 3, :], RT[0:32, 0, :], RT[0:32, 1, :], ALU.subtract))
                    nc.vector.tensor_tensor(RT[32:64, 2 + i % 3, :], RT[32:64, 0, :], RT[32:64, 1, :],
                                            ALU.add).then_inc(roped, 1)
                else:
                    dve.wait_ge(q_ready, j + 1)
                    qa, qb = PS[:, j % 2, :], PS[:, 2 + j % 2, :]
                    if t == 2:
                        qa, qb = qb, qa
                    step(nc.vector.tensor_tensor(RT[:, 0, :], qa, COS[:, tok], ALU.mult))
                    need(step(nc.vector.tensor_tensor(RT[:, 1, :], qb, SIN[:, tok], ALU.mult)))
                    nc.vector.tensor_tensor(RT[:, 2 + i % 3, :], RT[:, 0, :], RT[:, 1, :],
                                            ALU.subtract if t == 1 else ALU.add).then_inc(roped, 1)

            def remainder(i):
                j, t = divmod(i, 3)
                rows = 64 if t == 0 else P
                dve.wait_ge(hi_a, i + 1)
                if i >= 3:
                    dve.wait_ge(low_d, i - 2)
                nc.vector.tensor_tensor(RT[0:rows, 5 + i % 3, :], RT[0:rows, 2 + i % 3, :],
                                        PT[0:rows, j % 2, t, 0, :], ALU.subtract).then_inc(rem_d, 1)

            def low(i):
                j, t = divmod(i, 3)
                rows = 64 if t == 0 else P
                dve.wait_ge(mid_a, i + 1)
                nc.vector.tensor_tensor(PT[0:rows, j % 2, t, 2, :], RT[0:rows, 5 + i % 3, :],
                                        PT[0:rows, j % 2, t, 1, :], ALU.subtract).then_inc(low_d, 1)

            dve.wait_ge(tab_in, 32)
            for i in range(3 * NC + 2):
                if i < 3 * NC:
                    dve.wait_ge(roped, i) if i else None
                    rope(i)
                if 1 <= i <= 3 * NC:
                    remainder(i - 1)
                if i >= 2:
                    low(i - 2)

            dve.wait_ge(v_sb, 8)
            nc.vector.tensor_reduce(SC[:, 0:1], VF, AX.X, ALU.max, apply_absolute_value=True).then_inc(amax_d, 1)
            dve.wait_ge(wsum, 1)
            need(step(nc.vector.tensor_scalar(WS[:, 8:11], PS[:, 5, 0:3], 1.0 / (D * FF), 1e-8, ALU.mult, ALU.add)))
            nc.vector.reciprocal(WS[:, 12:15], WS[:, 8:11]).then_inc(wgam, 1)
            dve.wait_ge(aall_p, 1)
            need(step(nc.vector.tensor_scalar(SC[:, 2:3].bitcast(u32), SC[:, 1:2].bitcast(u32), 0x7f800000, None,
                                              ALU.bitwise_and)))
            need(step(nc.vector.tensor_scalar(SC[:, 3:4], SC[:, 2:3], 2.0 ** -100, 2.0 ** 126, ALU.max, ALU.min)))
            need(step(nc.vector.reciprocal(SC[:, 4:5], SC[:, 3:4])))
            step(nc.vector.tensor_scalar(SC[:, 6:7], SC[:, 3:4], 2.0 ** -13, None, ALU.mult))
            nc.vector.tensor_scalar(SC[:, 5:6], SC[:, 4:5], 2.0 ** 13, None, ALU.mult).then_inc(vscale, 1)
            dve.wait_ge(v_hi, 1)
            dve.wait_ge(vscale, 1)
            nc.vector.scalar_tensor_tensor(out=VP[:, :, :, DV + 1:VW - 1].rearrange("p t k e -> p (t k) e"),
                                           in0=VF.rearrange("p (a e) -> p a e", e=DV), scalar=SC[:, 5:6],
                                           in1=VP[:, :, :, 0:DV].rearrange("p t k e -> p (t k) e"),
                                           op0=ALU.mult, op1=ALU.subtract).then_inc(vp_ready, 1)

            def maximum(b, u):
                dve.wait_ge(x_ready, 16 * b + u + 1)
                if u == 0 and not (isinstance(b, int) and b == 0):
                    dve.wait_ge(nm_d, 5 * b - 4)
                nc.vector.tensor_reduce(MX[:, u // 4, u % 4:u % 4 + 1], PS[:, 4 + u % 2, :], AX.X,
                                        ALU.max).then_inc(x_read, 1)

            def split_max(b, k):
                if k == 0:
                    dve.wait_ge(x_read, 16 * b + 16)
                    ins = nc.vector.tensor_reduce(NM[:, :], MX[:, :, :], AX.X, ALU.max, negate=True)
                else:
                    dve.wait_ge(nm_d, 5 * b + k)
                    ins = (None,
                           lambda: nc.vector.tensor_copy(MP[:, :, 0], NM[:, :]),
                           lambda: nc.vector.tensor_tensor(R1[:, :], NM[:, :], MP[:, :, 0], ALU.subtract),
                           lambda: nc.vector.tensor_copy(MP[:, :, 1], R1[:, :]),
                           lambda: nc.vector.tensor_tensor(MP[:, :, 2], R1[:, :], MP[:, :, 1], ALU.subtract))[k]()
                ins.then_inc(nm_d, 1)

            def max_rows(b):
                dve.wait_ge(mt_ready, b + 1)
                nc.vector.tensor_copy(QC[MROW:MROW + 4, bass.ds(b, 1), :].rearrange("p o n -> p (o n)"),
                                      MT[MROW:MROW + 4, 0:512]).then_inc(m_rows, 1)

            def normalise(b, k):
                if k == 0:
                    dve.wait_ge(evac, b + 1)
                    ins = nc.vector.reciprocal(RR[:, :], EV[:, :, DV])
                elif k == 1:
                    ins = nc.vector.tensor_tensor(CS[:, :, :], EV[:, :, 0:DV], EV[:, :, DV + 1:129], ALU.add)
                else:
                    dve.wait_ge(norm_d, 3 * b + 2)
                    rr = RR[:, :].rearrange("p (i o) -> p i o", o=1).to_broadcast([P, 4, DV])
                    ins = nc.vector.scalar_tensor_tensor(
                        out=QF[:, bass.ds(b, 1), :, :].rearrange("p o i e -> p (o i) e"), in0=CS[:, :, :],
                        scalar=SC[:, 6:7], in1=rr, op0=ALU.mult, op1=ALU.mult)
                ins.then_inc(norm_d, 1)

            def dve_block(b, first=False, ahead=2):
                for s in range(STEPS):
                    t = 8 * b + s
                    dve.wait_ge(e_done, t + 1)
                    if not (first and s < 4):
                        dve.wait_ge(pv_done, t - 3)
                    nc.vector.tensor_tensor(PR[:, s % 4, POOLW:], PF[:, s % 4, POOLW:], PHI[:, s % 4, POOLW:],
                                            ALU.subtract).then_inc(r_dve, 1)
                    for n, (d, u) in enumerate(max_tiles(s)):
                        if d <= ahead:
                            maximum(b + d, u)
                        if ahead >= 1 and (s, n) in ((1, 1), (2, 0), (2, 1), (3, 0), (3, 1)):
                            split_max(b + 1, 2 * s + n - 3)
                    if s == 4 and ahead >= 1:
                        max_rows(b + 1)
                    if not first and s in (2, 3, 4):
                        normalise(b - 1, s - 2)

            for u in range(16):
                maximum(0, u)
            for k in range(5):
                split_max(0, k)
            max_rows(0)
            for u in range(12):
                maximum(1, u)
            dve_block(0, first=True)
            with dve.Fori(1, NB - 2) as b:
                dve_block(b)
            dve_block(NB - 2, ahead=1)
            dve_block(NB - 1, ahead=0)
            for k in range(3):
                normalise(NB - 1, k)

            count_before = count[0]
            assert count_before == DCH_BEFORE_END, count_before
            dve.wait_ge(bo_in, 16)
            for hp in range(2):
                context_half(dve, nc.vector.tensor_copy, ct_d, 0, 1, hp)
            for n in range(NT):
                if n % 2 == 0 and n < NT - 2:
                    for hp in range(2):
                        context_half(dve, nc.vector.tensor_copy, ct_d, n // 2 + 1, 1, hp)
                dve.wait_ge(y_ready, n + 1)
                nc.vector.tensor_tensor(XS[:, n, :], XS[:, n, :], PS[:, 4 + n % 2, 0:D], ALU.add).then_inc(y_read, 1)
                dve.wait_ge(y_read, n + 1)
                need(step(nc.vector.tensor_tensor(XS[:, n, :], XS[:, n, :], BO[:, :], ALU.add)))
                need(step(nc.vector.bn_stats(ST[:, n, :], XS[:, n, :])))
                step(nc.vector.bn_aggr(MV[:, n, :], ST[:, n, :]))
            need(count[0])
            rstd(std2_a, LN2_VAR)
            for n in range(NT):
                nc.vector.tensor_scalar(X2[:, n, :], XS[:, n, :], MV[:, n, 0:1], RS[:, 5, n:n + 1],
                                        ALU.subtract, ALU.mult).then_inc(x2_ready, 1)
            for i in range(2 * NC):
                dve.wait_ge(t2_hi, i + 1)
                tok = slice((i // 2) * 512, (i // 2) * 512 + 512)
                nc.vector.tensor_tensor(T2L[:, i % 2, tok], PS[:, i, :], T2H[:, i % 2, tok],
                                        ALU.subtract).then_inc(t2_lo, 1)
            NG = NC * len(FCH)

            def hidden_lo(i):
                j, f = divmod(i, len(FCH))
                rows = FCH[f][1]
                dve.wait_ge(hh_a, i + 1)
                nc.vector.tensor_tensor(HP[0:rows, j % 2, 1, f, :], HD[0:rows, i % 4, :], HP[0:rows, j % 2, 0, f, :],
                                        ALU.subtract).then_inc(hl_d, 1)

            def results(j):
                for i in range(4):
                    n = 4 * j + i
                    dve.wait_ge(o_ready, n + 1)
                    nc.vector.tensor_tensor(XS[:, n, :], XS[:, n, :], PS[:, 6 + n % 2, 0:D], ALU.add).then_inc(o_sb, 1)

            for i in range(NG):
                rows = FCH[i % len(FCH)][1]
                dve.wait_ge(sig_a, i + 1)
                if i >= 4:
                    dve.wait_ge(hl_d, i - 3)
                nc.vector.tensor_tensor(HD[0:rows, i % 4, :], SG[0:rows, i % 2, :], PS[0:rows, 2 * (i % 3) + 1, :],
                                        ALU.mult).then_inc(hid_d, 1)
                if i >= 1:
                    hidden_lo(i - 1)
                if i % len(FCH) == len(FCH) - 1 and i >= len(FCH):
                    results(i // len(FCH) - 1)
            hidden_lo(NG - 1)
            results(NC - 1)

        @block.tensor
        def _(pe):
            pe.wait_ge(id_in, 16)
            for j in range(NC):
                for i in range(4):
                    n = 4 * j + i
                    pe.wait_ge(xn_ready, n + 1)
                    for c in range(DC):
                        last = nc.tensor.transpose(PS[:, 2 * j + c, i * P:(i + 1) * P], XN[:, n, c * P:(c + 1) * P],
                                                   ID[:])
                last.then_inc(tr_ready, 1)
            pe.wait_ge(wq_in, 16)
            pe.wait_ge(xnt_a, NC)
            pe.wait_ge(xnt_d, NC)
            for j in range(NC):
                tok = slice(j * 512, (j + 1) * 512)
                if j >= 2:
                    pe.wait_ge(roped, 3 * (j - 2) + 3)
                for name, bank, col, width in (("k", 4 + j % 2, 0, 64), ("a", j % 2, 64, P), ("b", 2 + j % 2, 192, P)):
                    for c in range(DC):
                        last = nc.tensor.matmul(PS[0:width, bank, :], WQ[:, c, col:col + width], XNT[:, c, tok],
                                                start=c == 0, stop=c == DC - 1)
                    if name == "k":
                        last.then_inc(k_ready, 1)
                last.then_inc(q_ready, 1)
                for n in range(2):
                    if j >= 1:
                        pe.wait_ge(v_sb, 2 * (j - 1) + n + 1)
                    for i in range(2):
                        tt = 4 * j + 2 * n + i
                        for c in range(DC):
                            last = nc.tensor.matmul(PS[:, 6 + n, i * D:(i + 1) * D], XNT[:, c, tt * P:(tt + 1) * P],
                                                    WQ[:, c, 320:576], start=c == 0, stop=c == DC - 1)
                    last.then_inc(v_ready, 1)
            pe.wait_ge(ones_set, 1)
            pe.wait_ge(wabs, 3)
            pe.wait_ge(roped, 3 * NC)
            nc.tensor.matmul(PS[:, 5, 0:3], ONES[:], WS[:, 0:3], start=True, stop=True).then_inc(wsum, 1)

            def max_tile(b, u):
                i, c = divmod(u, 4)
                if not (isinstance(b, int) and b == 0 and u < 2):
                    pe.wait_ge(x_read, 16 * b + u - 1)
                nc.tensor.matmul(PS[:, 4 + u % 2, :],
                                 QC[0:KROWS, bass.ds(b, 1), i * P:(i + 1) * P].rearrange("p o n -> p (o n)"),
                                 KA[0:KROWS, bass.ds(kv_of(b) * L + c * 512, 512)],
                                 start=True, stop=True).then_inc(x_ready, 1)

            def max_transposes(b):
                pe.wait_ge(nm_d, 5 * b + 5)
                for i in range(4):
                    last = nc.tensor.transpose(MT[MROW:MROW + 4, i * P:(i + 1) * P], MP[:, i, :], IDB[:])
                last.then_inc(mt_ready, 1)

            def scores(b, s):
                for k in range(2):
                    last = nc.tensor.matmul(SCO[:, 2 * (s % 2) + k, :],
                                            KA[0:QROWS, bass.ds(kv_of(b) * L + (2 * s + k) * P, P)],
                                            QC[0:QROWS, bass.ds(b, 1), :].rearrange("p o n -> p (o n)"),
                                            start=True, stop=True)
                last.then_inc(s_ready, 1)

            def product(b, s, k):
                for i in range(4):
                    col = k * 512 + i * P
                    for w, (p, cols) in enumerate(((PHI, 129), (PR, PRW))):
                        last = nc.tensor.matmul(
                            ACC[:, i, 0:cols], p[:, s % 4, col:col + P],
                            VP[:, 2 * s + k, bass.ds(kv_of(b), 1), 0:cols].rearrange("p o e -> p (o e)"),
                            start=(s == 0 and k == 0 and i % 2 == 0 and w == 0),
                            stop=(s == STEPS - 1 and k == 1 and w == 1), skip_group_check=True)
                return last

            def pe_block(b, first=False, ahead=2):
                for s in range(STEPS):
                    t = 8 * b + s
                    if s < STEPS - 2 or ahead >= 1:
                        pe.wait_ge(e_done, t + 1)
                        if s < STEPS - 2:
                            scores(b, s + 2)
                        else:
                            if s == STEPS - 2:
                                pe.wait_ge(m_rows, b + 2)
                            scores(b + 1, s - (STEPS - 2))
                    for n, (d, u) in enumerate(max_tiles(s)):
                        if d <= ahead:
                            if s == 5 and n == 0:
                                pe.wait_ge(m_rows, b + 2)
                            max_tile(b + d, u)
                    if s == 0 and not first:
                        pe.wait_ge(evac, b)
                    pe.wait_ge(r_pool, t + 1)
                    product(b, s, 0)
                    if s == 4 and ahead >= 1:
                        if ahead >= 2:
                            pe.wait_ge(x_read, 16 * (b + 2) + 5)
                        max_transposes(b + 1)
                    pe.wait_ge(r_dve, t + 1)
                    product(b, s, 1).then_inc(pv_done, 1)

            pe.wait_ge(ops_in, 16 * 24)
            pe.wait_ge(k_ones, 1)
            pe.wait_ge(idb_set, 1)
            pe.wait_ge(cst_set, 2)
            pe.wait_ge(wgam, 1)
            for u in range(16):
                max_tile(0, u)
            pe.wait_ge(x_read, 16)
            max_transposes(0)
            pe.wait_ge(m_rows, 1)
            for u in range(12):
                max_tile(1, u)
                if u in (0, 6):
                    scores(0, u // 6)
            pe.wait_ge(vp_ready, 1)
            pe_block(0, first=True)
            with pe.Fori(1, NB - 2) as b:
                pe_block(b)
            pe_block(NB - 2, ahead=1)
            pe_block(NB - 1, ahead=0)

            def turn(m):
                if m >= 1:
                    pe.wait_ge(ct_a, 2 * m)
                    pe.wait_ge(ct_d, 2 * m)
                for h in range(NH):
                    hp, c = h % 2, h // 2
                    last = nc.tensor.transpose(
                        PS[:, 2 * hp + c // 4, (c % 4) * P:(c % 4 + 1) * P],
                        QF[:, h * NC + m // 2, 2 * (m % 2):2 * (m % 2) + 2, :].rearrange("p i e -> p (i e)"), ID[:])
                last.then_inc(ct_ready, 1)

            def project(n):
                if n % 2 == 0:
                    pe.wait_ge(ct_a, n + 2)
                    pe.wait_ge(ct_d, n + 2)
                if n >= 2:
                    pe.wait_ge(y_read, n - 1)
                for c in range(OC):
                    last = nc.tensor.matmul(PS[:, 4 + n % 2, 0:D], CT[:, n // 2 % 2, n % 2, c, :], WO[:, c, :],
                                            start=c == 0, stop=c == OC - 1)
                last.then_inc(y_ready, 1)

            pe.wait_ge(norm_d, 3 * NB)
            pe.wait_ge(wo_in, 16)
            turn(0)
            for m in range(NT // 2):
                if m + 1 < NT // 2:
                    turn(m + 1)
                project(2 * m)
                project(2 * m + 1)
            pe.wait_ge(y_read, NT)
            for j in range(NC):
                for i in range(4):
                    n = 4 * j + i
                    pe.wait_ge(x2_ready, n + 1)
                    for c in range(DC):
                        last = nc.tensor.transpose(PS[:, 2 * j + c, i * P:(i + 1) * P], X2[:, n, c * P:(c + 1) * P],
                                                   ID[:])
                        if i == 3:
                            last.then_inc(t2_ready, 1)
            pe.wait_ge(t2_lo, 2 * NC)

            def up(i):
                j, f = divmod(i, len(FCH))
                h0, rows = FCH[f]
                tok = slice(j * 512, (j + 1) * 512)
                if i >= 3:
                    pe.wait_ge(hid_d, i - 2)
                for w, wq in enumerate((W1Q, W2Q)):
                    for c in range(DC):
                        for k, part in enumerate((T2H, T2L)):
                            last = nc.tensor.matmul(PS[0:rows, 2 * (i % 3) + w, :], wq[:, c, h0:h0 + rows],
                                                    part[:, c, tok], start=(c == 0 and k == 0),
                                                    stop=(c == DC - 1 and k == 1))
                last.then_inc(g_ready, 1)

            def down(j):
                pe.wait_ge(hl_d, (j + 1) * len(FCH))
                for i in range(4):
                    n = 4 * j + i
                    if n >= 2:
                        pe.wait_ge(o_sb, n - 1)
                    for f, (_, rows) in enumerate(FCH):
                        for k in range(2):
                            last = nc.tensor.matmul(PS[:, 6 + n % 2, 0:D], HP[0:rows, j % 2, k, f, i * P:(i + 1) * P],
                                                    W3Q[0:rows, f, :], start=(f == 0 and k == 0),
                                                    stop=(f == len(FCH) - 1 and k == 1))
                    last.then_inc(o_ready, 1)

            pe.wait_ge(pch, 10)
            for j in range(NC):
                for f in range(len(FCH)):
                    up(j * len(FCH) + f)
                if j >= 1:
                    down(j - 1)
            down(NC - 1)


def kernel(**inputs):
    import concourse.bacc as bacc
    from concourse.bass_utils import run_bass_kernel_spmd

    def arr(name):
        return np.ascontiguousarray(inputs["L0_" + name])

    w = arr("attn_W_attn")
    qd, kd = NH * DK, NKV * DK
    qcols = np.arange(qd).reshape(NH, 2, HF)
    kcols = qd + np.arange(kd).reshape(NKV, 2, HF)
    order = np.concatenate([kcols[:, 0].ravel(), kcols[:, 1].ravel(), qcols[:, 0].ravel(), qcols[:, 1].ravel(),
                            np.arange(qd + kd, w.shape[1])])
    inv = (np.float32(1.0) / np.float32(10000.0) ** (np.arange(0, DK, 2, dtype=np.float32) / np.float32(DK)))
    ang = inv.astype(np.float32)[:, None] * np.arange(L, dtype=np.float32)[None, :]
    half = np.float32(DK ** -0.25)
    arrays = {
        "x": arr("attn_x").reshape(L, D),
        "w_qkv": np.ascontiguousarray(w[:, order]),
        "w_out": arr("attn_W_out"),
        "b_out": arr("attn_b_out").reshape(1, D),
        "w1t": np.ascontiguousarray(arr("ffn_w1").T),
        "w2t": np.ascontiguousarray(arr("ffn_w2").T),
        "w3t": np.ascontiguousarray(arr("ffn_w3").T),
        "cos_t": np.tile(np.cos(ang) * half, (P // HF, 1)),
        "sin_t": np.tile(np.sin(ang) * half, (P // HF, 1)),
        "ident": np.eye(P, dtype=np.float32),
    }
    nc = bacc.Bacc("TRN2", target_bir_lowering=False, num_devices=1)
    args = [nc.dram_tensor(n + "_dram", a.shape, fp32, kind="ExternalInput").ap() for n, a in arrays.items()]
    out = nc.dram_tensor("out_dram", (L, D), fp32, kind="ExternalOutput").ap()
    layer(nc, *args, out)
    r = run_bass_kernel_spmd(nc, [{n + "_dram": a for n, a in arrays.items()}], core_ids=[0])
    return r.results[0]["out_dram"].reshape(1, L, D)
```

```python
import concourse.bass as bass
from concourse import mybir
from contextlib import ExitStack
import numpy as np

fp32 = mybir.dt.float32
bf16 = mybir.dt.bfloat16
fp16 = mybir.dt.float16
u32 = mybir.dt.uint32
ALU = mybir.AluOpType
ACT = mybir.ActivationFunctionType
AX = mybir.AxisListType

L, D = 2048, 256
NH, NKV, DK, DV = 16, 4, 16, 64
HF = DK // 2
FF = 704
P = 128
NT = L // P
NC = L // 512
DC = D // P
NB = NH * NC
STEPS = NT // 2
KROWS = 6 * DK
MROW = KROWS
QROWS = KROWS + 4
SHIFT = 8.3125
VW = 130
POOLW = 736
FCH = [(i * P, min(P, FF - i * P)) for i in range((FF + P - 1) // P)]
OC = NH * DV // P
AHEAD = 14
PRW = 129
NR = NC * 3
PSLOTS = 6
TERMS = [(0, 0), (0, 1), (1, 0), (1, 1), (0, 2), (2, 0)]


def layer(nc, x, w_qkv, w_out, b_out, w1t, w2t, w3t, cos_t, sin_t, ksin_t, ident, out):
    q_parts = nc.dram_tensor("q_parts", (3, NH, 2, HF, L), bf16, kind="Internal").ap()
    k_parts = nc.dram_tensor("k_parts", (3, NKV * DK, L), bf16, kind="Internal").ap()

    ctx = ExitStack()
    with ctx:
        def sb(name, shape, dt):
            return ctx.enter_context(nc.sbuf_tensor(name, shape, dt))

        def sem(name):
            return ctx.enter_context(nc.semaphore(name))

        QC = sb("QC", [P, NB, 512], bf16)
        KA = sb("KA", [P, NKV * L], bf16)
        VP = sb("VP", [P, NT, NKV, VW], fp16)
        PF = sb("PF", [P, 4, 1024], fp32)
        PR = sb("PR", [P, 4, 1024], fp16)
        MX = sb("MX", [P, 4, 4], fp32)
        NM = sb("NM", [P, 4], fp32)
        R1 = sb("R1", [P, 4], fp32)
        MP = sb("MP", [P, 4, 4], bf16)
        EV = sb("EV", [P, 4, 129], fp32)
        CS = sb("CS", [P, 4, DV], fp32)
        RR = sb("RR", [P, 4], fp32)
        XS = sb("XS", [P, NT, D], fp32)
        WO = sb("WO", [P, OC, D], fp32)
        WT = sb("WT", [P, 2 * DC * FF + len(FCH) * D], fp16)
        W1Q = WT[:, 0:DC * FF].rearrange("p (c n) -> p c n", c=DC)
        W2Q = WT[:, DC * FF:2 * DC * FF].rearrange("p (c n) -> p c n", c=DC)
        W3Q = WT[:, 2 * DC * FF:].rearrange("p (c n) -> p c n", c=len(FCH))
        PT = sb("PT", [P, PSLOTS, 3, 512], bf16)
        XNT = sb("XNT", [P, DC, L], fp32)
        ID = sb("ID", [P, P], fp32)
        IDB = sb("IDB", [P, P], bf16)
        ONES = sb("ONES", [P, P], fp32)
        BO = sb("BO", [P, D], fp32)
        ST = sb("ST", [P, NT, 6], fp32)
        MV = sb("MV", [P, NT, 2], fp32)
        RS = sb("RS", [P, 6, NT], fp32)
        WS = sb("WS", [P, 16], fp32)
        AM = sb("AM", [P, 2], fp32)
        SC = sb("SC", [P, 8], fp32)

        QCF = QC[:, :, :].rearrange("p b n -> p (b n)").bitcast(fp32)
        XN = PF[:, :, :].rearrange("p a b -> p (a b)").rearrange("p (t n) -> p t n", t=NT)
        VF = PF[:, :, :].rearrange("p a b -> p (a b)")
        COS = WO[:, :, :].rearrange("p c n -> p (c n)")
        SIN = WT[:, 0:2 * L].bitcast(fp32)
        KSIN = QCF[:, 8192:10240]
        RT = QCF[:, 10240:15360].rearrange("p (s n) -> p s n", n=512)
        WQ = PR[:, :, :].rearrange("p a b -> p (a b)").bitcast(fp32)[:, 0:1280].rearrange("p (c n) -> p c n", c=DC)
        QF = QC[:, :, :].rearrange("p b n -> p (b n)").bitcast(fp32).rearrange("p (b i e) -> p b i e", b=NB, i=4)
        CT = KA[:, :].bitcast(fp32).rearrange("p (r i c t) -> p r i c t", r=2, i=2, c=OC)
        X2 = PF[:, :, :].rearrange("p a b -> p (a b)").rearrange("p (t n) -> p t n", t=NT)
        T2H = PR[:, :, :].rearrange("p a b -> p (a b)").rearrange("p (c t) -> p c t", c=DC)
        T2L = XNT[:, 0, :].bitcast(fp16).rearrange("p (c t) -> p c t", c=DC)
        HP = QCF[:, 0:6144].bitcast(fp16).rearrange("p (r q f t) -> p r q f t", r=2, q=2, f=len(FCH))
        SG = QCF[:, 8192:9216].rearrange("p (r t) -> p r t", r=2)
        HD = QCF[:, 9216:11264].rearrange("p (r t) -> p r t", r=4)
        PHI = PF[:, :, :].rearrange("p a b -> p (a b)").bitcast(bf16)\
            .rearrange("p (a b two) -> p a b two", a=4, two=2)[:, :, :, 1]
        PTF = PT[:, :, :, :].rearrange("p a b c -> p (a b c)").bitcast(fp32)
        RW1, RW2, RW3 = PTF[:, 0:DC * FF], PTF[:, DC * FF:2 * DC * FF], \
            PTF[:, 2 * DC * FF:2 * DC * FF + len(FCH) * D]

        PS = ctx.enter_context(nc.psum_tensor("PS", [P, 8, 512], fp32))
        SCO = PS[:, 0:4, :]
        ACC = PS[:, 6:8, :].rearrange("p b (i n) -> p (b i) n", i=2)
        MT = PS[:, 4, :].bitcast(bf16)

        xin = [sem(f"xin{j}") for j in range(NC)]
        (wq_in, k_tab_in, q_tab_in, id_in, bo_in, wo_in) = map(sem, (
            "wq_in", "k_tab_in", "q_tab_in", "id_in", "bo_in", "wo_in"))
        rw_in = [sem(f"rw_in{i}") for i in range(3)]
        (ones_set, idb_set, cst_set) = map(sem, ("ones_set", "idb_set", "cst_set"))
        dch = sem("dch")
        (std_a, xn_ready, tr_ready, xnt_a, rw_zero) = map(sem, ("std_a", "xn_ready", "tr_ready", "xnt_a", "rw_zero"))
        (k_ready, q_ready, v_ready, v_sb, roped, hi_a, rem_p, mid_a, low_p) = map(sem, (
            "k_ready", "q_ready", "v_ready", "v_sb", "roped", "hi_a", "rem_p", "mid_a", "low_p"))
        parts_out = [sem(f"parts_out{i}") for i in range(PSLOTS)]
        q_in = [sem(f"q_in{j}") for j in range(NC + 1)]
        (k_in, k_ones, amax_d, aall_p, vscale, v_hi, vp_ready) = map(sem, (
            "k_in", "k_ones", "amax_d", "aall_p", "vscale", "v_hi", "vp_ready"))
        (wabs, wsum, wgam, w_tern) = map(sem, ("wabs", "wsum", "wgam", "w_tern"))
        s_ready = sem("s_ready")
        e_done = sem("e_done")
        x_ready = sem("x_ready")
        x_read = sem("x_read")
        nm_d = sem("nm_d")
        mt_ready = sem("mt_ready")
        m_rows = sem("m_rows")
        r_pool = sem("r_pool")
        r_dve = sem("r_dve")
        pv_done = sem("pv_done")
        evac = sem("evac")
        rr_d = sem("rr_d")
        cs_p = sem("cs_p")
        norm_d = sem("norm_d")
        (var_d, bo_p) = map(sem, ("var_d", "bo_p"))
        (ct_ready, ct_a, ct_d, y_ready, y_read, t2_ready, t2_hi, t2_lo) = map(sem, (
            "ct_ready", "ct_a", "ct_d", "y_ready", "y_read", "t2_ready", "t2_hi", "t2_lo"))
        (x2_ready, std2_a, g_ready, sig_a, hid_d, hh_a, hl_d, o_ready, o_sb, o_out) = map(sem, (
            "x2_ready", "std2_a", "g_ready", "sig_a", "hid_d", "hh_a", "hl_d", "o_ready", "o_sb", "o_out"))
        block = ctx.enter_context(nc.Block())

        def kv_of(b):
            return b // (NB // NKV)

        def max_tiles(s):
            return [(1 if s < 1 else 2, (2 * s + AHEAD) % 16 + n) for n in range(2)]

        def rotated(i):
            return (None, i, 64) if i < NC else ((i - NC) % 2, (i - NC) // 2, P)

        def q_bank(j, half):
            return (6, 0, 2, 0)[j] + half

        def sent(i):
            before = [16 * (1 if n < NC else 3) for n in range(i % PSLOTS, i + 1, PSLOTS)]
            return parts_out[i % PSLOTS], sum(before)

        def v_part(h, at):
            return VP[:, h * NT // 2:(h + 1) * NT // 2, :, at:at + DV].rearrange("p t k e -> p (t k) e")

        def v_float(h):
            return VF[:, h * 2048:(h + 1) * 2048].rearrange("p (a e) -> p a e", e=DV)

        def context_half(eng, copy, done, m, i, hp):
            eng.wait_ge(ct_ready, m + 1)
            if m >= 2 and hp == 0:
                eng.wait_ge(y_ready, 2 * (m - 1))
            copy(CT[64 * hp:64 * hp + 64, m % 2, i, :, :].rearrange("p (b c) t -> p b (c t)", b=2),
                 PS[64 * i:64 * i + 64, 2 * hp:2 * hp + 2, :]).then_inc(done, 1)

        @block.sync
        def _(sp):
            for j in range(NC):
                sp.dma_start(XS[:, 4 * j:4 * j + 4, :],
                             x[j * 512:(j + 1) * 512, :].rearrange("(t p) d -> p t d", p=P)).then_inc(xin[j], 16)
                if j == 0:
                    sp.dma_start(ID[:], ident).then_inc(id_in, 16)
                    sp.dma_start(WQ, w_qkv.rearrange("(c p) n -> p c n", p=P)).then_inc(wq_in, 16)
                if j == 1:
                    sp.dma_start(COS[0:64, :], cos_t[0:64, :]).then_inc(k_tab_in, 16)
                    sp.dma_start(KSIN[64:128, :], ksin_t).then_inc(k_tab_in, 16)
            sp.dma_start(COS[64:128, :], cos_t[64:128, :]).then_inc(q_tab_in, 16)
            sp.dma_start(SIN, sin_t).then_inc(q_tab_in, 16)
            sp.dma_start(BO[:], b_out.partition_broadcast(P)).then_inc(bo_in, 16)

            def send(i):
                half, j, _ = rotated(i)
                tok = slice(j * 512, (j + 1) * 512)
                sp.wait_ge(low_p, i + 1)
                if half is None:
                    sp.dma_start(k_parts[:, :, tok].rearrange("q r n -> r q n"), PT[0:64, i % PSLOTS, :, :]
                                 ).then_inc(parts_out[i % PSLOTS], 16)
                else:
                    for q in range(3):
                        sp.dma_start(q_parts[q, :, half, :, tok], PT[:, i % PSLOTS, q, :]
                                     ).then_inc(parts_out[i % PSLOTS], 16)

            def rows_of(g):
                return slice(DK * g, DK * (g + 1))

            for i in range(NC):
                send(i)
            for i in range(NC):
                sp.wait_ge(*sent(i))
            for g, (_, kp) in enumerate(TERMS):
                sp.dma_start(KA[rows_of(g), :].rearrange("r (k t) -> r k t", k=NKV),
                             k_parts[kp].rearrange("(k r) t -> r k t", k=NKV)).then_inc(k_in, 16)
            heads = NH // 2
            for j in range(NC):
                for i in range(NC + (2 * j + 1 if j else 0), min(NC + 2 * j + 3, NR)):
                    send(i)
                for i in (NC + 2 * j, NC + 2 * j + 1):
                    sp.wait_ge(*sent(i))
                for g, (qp, _) in enumerate(TERMS):
                    sp.dma_start(QC[rows_of(g), j:heads * NC:NC, :],
                                 q_parts[qp, 0:heads, :, :, j * 512:(j + 1) * 512]
                                 .rearrange("a h f t -> (h f) a t")).then_inc(q_in[j], 16)
            for g, (qp, _) in enumerate(TERMS):
                sp.dma_start(QC[rows_of(g), heads * NC:, :].rearrange("r (a b) n -> r a (b n)", a=heads),
                             q_parts[qp, heads:].rearrange("a h f t -> (h f) a t")).then_inc(q_in[NC], 16)
            sp.dma_start(WO[:, :, :], w_out.rearrange("(c p) n -> p c n", p=P)).then_inc(wo_in, 16)
            sp.dma_start(RW1.rearrange("p (c n) -> p c n", c=DC),
                         w1t.rearrange("(c p) n -> p c n", p=P)).then_inc(rw_in[0], 16)
            sp.dma_start(RW2.rearrange("p (c n) -> p c n", c=DC),
                         w2t.rearrange("(c p) n -> p c n", p=P)).then_inc(rw_in[1], 16)
            nf = FF // P
            sp.dma_start(RW3[:, 0:nf * D].rearrange("p (c n) -> p c n", c=nf),
                         w3t[0:nf * P, :].rearrange("(c p) n -> p c n", p=P)).then_inc(rw_in[2], 16)
            sp.dma_start(RW3[0:FF - nf * P, nf * D:], w3t[nf * P:, :]).then_inc(rw_in[2], 16)
            for n in range(NT):
                sp.wait_ge(o_sb, n + 1)
                sp.dma_start(out[n * P:(n + 1) * P, :], XS[:, n, :]).then_inc(o_out, 16)
            sp.wait_ge(o_out, 16 * NT)

        @block.gpsimd
        def _(pool):
            nc.gpsimd.memset(KA[MROW:MROW + 4, :], 1.0).then_inc(k_ones, 1)
            pool.wait_ge(k_ones, 1)
            nc.gpsimd.memset(ONES[:], 1.0).then_inc(ones_set, 1)
            nc.gpsimd.memset(VP[:, :, :, DV:DV + 1], 1.0).then_inc(cst_set, 1)
            nc.gpsimd.memset(MP[:, :, 3:4], SHIFT).then_inc(cst_set, 1)
            pool.wait_ge(cst_set, 2)

            def remainder(i):
                _, _, rows = rotated(i)
                pool.wait_ge(hi_a, i + 1)
                if i >= 3:
                    pool.wait_ge(low_p, i - 2)
                nc.gpsimd.tensor_tensor(RT[0:rows, 7 + i % 3, :], RT[0:rows, 4 + i % 3, :],
                                        PT[0:rows, i % PSLOTS, 0, :], ALU.subtract).then_inc(rem_p, 1)

            def low(i):
                _, _, rows = rotated(i)
                pool.wait_ge(mid_a, i + 1)
                nc.gpsimd.tensor_tensor(PT[0:rows, i % PSLOTS, 2, :], RT[0:rows, 7 + i % 3, :],
                                        PT[0:rows, i % PSLOTS, 1, :], ALU.subtract).then_inc(low_p, 1)

            for i in range(NR + 1):
                if i < NR:
                    remainder(i)
                if i >= 1:
                    low(i - 1)
            pool.wait_ge(amax_d, 1)
            nc.gpsimd.partition_all_reduce(SC[:, 1:2], SC[:, 0:1], P, bass.bass_isa.ReduceOp.max).then_inc(aall_p, 1)
            pool.wait_ge(aall_p, 1)
            for i in range(NR - PSLOTS, NR):
                pool.wait_ge(*sent(i))
            nc.gpsimd.memset(RW3[64:128, (FF // P) * D:], 0.0).then_inc(rw_zero, 1)
            pool.wait_ge(rw_zero, 1)

            def pool_block(b, first=False):
                for s in range(STEPS):
                    t = 8 * b + s
                    pool.wait_ge(e_done, t + 1)
                    if not (first and s < 4):
                        pool.wait_ge(pv_done, t - 3)
                    nc.gpsimd.tensor_tensor(PR[:, s % 4, 0:POOLW], PF[:, s % 4, 0:POOLW], PHI[:, s % 4, 0:POOLW],
                                            ALU.subtract).then_inc(r_pool, 1)
                    if s == 3 and not first:
                        add_parts(b - 1)

            def add_parts(b):
                pool.wait_ge(evac, b + 1)
                nc.gpsimd.tensor_tensor(CS[:, :, :], EV[:, :, 0:DV], EV[:, :, DV + 1:129], ALU.add).then_inc(cs_p, 1)

            pool_block(0, first=True)
            with pool.Fori(1, NB - 2) as b:
                pool_block(b)
            pool_block(NB - 2)
            pool_block(NB - 1)
            add_parts(NB - 1)
            pool.wait_ge(bo_in, 16)
            for n in range(NT):
                nc.gpsimd.tensor_tensor(XS[:, n, :], XS[:, n, :], BO[:, :], ALU.add).then_inc(bo_p, 1)

        @block.scalar
        def _(act):
            def hi(i):
                _, _, rows = rotated(i)
                act.wait_ge(roped, i + 1)
                if i >= PSLOTS:
                    act.wait_ge(*sent(i - PSLOTS))
                nc.scalar.copy(PT[0:rows, i % PSLOTS, 0, :], RT[0:rows, 4 + i % 3, :]).then_inc(hi_a, 1)

            def mid(i):
                _, _, rows = rotated(i)
                act.wait_ge(rem_p, i + 1)
                nc.scalar.copy(PT[0:rows, i % PSLOTS, 1, :], RT[0:rows, 7 + i % 3, :]).then_inc(mid_a, 1)

            def v_out(n):
                act.wait_ge(v_ready, n + 1)
                nc.scalar.copy(VF[:, n * 512:(n + 1) * 512], PS[:, 6 + n % 2, :]).then_inc(v_sb, 1)

            def v_high(h):
                act.wait_ge(vscale, 1)
                nc.scalar.activation(v_part(h, 0), v_float(h), ACT.Copy, scale=SC[:, 5:6]).then_inc(v_hi, 1)

            def square_root(j, done):
                act.wait_ge(var_d, len(sqrts) + 1)
                nc.scalar.activation(RS[:, 1, 4 * j:4 * j + 4], RS[:, 0, 4 * j:4 * j + 4], ACT.Sqrt).then_inc(done, 1)
                sqrts.append(j)

            sqrts = []
            for j in range(NC):
                square_root(j, std_a)
                act.wait_ge(tr_ready, j + 1)
                for c in range(DC):
                    nc.scalar.copy(XNT[:, c, j * 512:(j + 1) * 512], PS[:, 2 * (j % 2) + c, :]).then_inc(xnt_a, 1)
                if j >= 1:
                    hi(j - 1)
                if j >= 2:
                    mid(j - 2)
            hi(NC - 1)
            mid(NC - 2)
            for i in range(NC, NR):
                hi(i)
                mid(i - 1)
                v_out(i - NC)
            mid(NR - 1)

            def take_out(b):
                act.wait_ge(pv_done, 8 * b + 8)
                nc.scalar.copy(EV[:, :, :], ACC[:, :, 0:129]).then_inc(evac, 1)

            def max_rows(b):
                act.wait_ge(mt_ready, b + 1)
                nc.scalar.copy(QC[MROW:MROW + 4, bass.ds(b, 1), :].rearrange("p o n -> p (o n)"),
                               MT[MROW:MROW + 4, 0:512]).then_inc(m_rows, 1)

            def act_block(b, first=False, ahead=2):
                for s in range(STEPS):
                    t = 8 * b + s
                    act.wait_ge(s_ready, t + 1)
                    if first and s in (0, 2):
                        act.wait_ge(vp_ready, 1 + s // 2)
                    if not (first and s < 4):
                        act.wait_ge(pv_done, t - 3)
                    nc.scalar.activation(PF[:, s % 4, :].rearrange("p (k n) -> p k n", k=2),
                                         SCO[:, 2 * (s % 2):2 * (s % 2) + 2, :], ACT.Exp).then_inc(e_done, 1)
                    if s == 1 and not first:
                        take_out(b - 1)
                    if s == 6 and ahead >= 1:
                        max_rows(b + 1)

            for h in range(2):
                v_high(h)
            nc.scalar.activation(WS[:, 15:16], SC[:, 5:6], ACT.Exp, scale=0.0)
            max_rows(0)
            act_block(0, first=True)
            with act.Fori(1, NB - 2) as b:
                act_block(b)
            act_block(NB - 2, ahead=1)
            act_block(NB - 1, ahead=0)
            take_out(NB - 1)

            w_abs = (W1Q, W2Q, W3Q)

            def norm_high(j):
                for c in range(DC):
                    act.wait_ge(t2_ready, 2 * j + c + 1)
                    nc.scalar.copy(T2H[:, c, j * 512:(j + 1) * 512], PS[:, 6 + c, :]).then_inc(t2_hi, 1)

            for m in range(NT // 2):
                for hp in range(2):
                    context_half(act, nc.scalar.copy, ct_a, m, 0, hp)
                if m < 3:
                    act.wait_ge(rw_in[m], 16 if m < 2 else 32)
                    if m == 2:
                        act.wait_ge(rw_zero, 1)
                    nc.scalar.activation(w_abs[m].rearrange("p c n -> p (c n)").bitcast(bf16), (RW1, RW2, RW3)[m],
                                         ACT.Abs, accum_out=WS[:, m:m + 1]).then_inc(wabs, 1)
                if m % 2 == 0 and m >= 2:
                    square_root(m // 2 - 1, std2_a)
                if m % 2 == 1 and m >= 3:
                    norm_high(m // 2 - 1)
            square_root(NC - 1, std2_a)
            def hidden_hi(i):
                j, f = divmod(i, len(FCH))
                act.wait_ge(hid_d, i + 1)
                if j >= 2:
                    act.wait_ge(o_ready, 4 * (j - 1))
                rows = FCH[f][1]
                nc.scalar.copy(HP[0:rows, j % 2, 0, f, :], HD[0:rows, i % 4, :]).then_inc(hh_a, 1)

            NG = NC * len(FCH)
            for i in range(NG + 1):
                if i == 2:
                    norm_high(NC - 1)
                if i < NG:
                    rows = FCH[i % len(FCH)][1]
                    act.wait_ge(g_ready, i + 1)
                    if i >= 2:
                        act.wait_ge(hid_d, i - 1)
                    nc.scalar.activation(SG[0:rows, i % 2, :], PS[0:rows, 2 * (i % 3), :],
                                         ACT.Sigmoid).then_inc(sig_a, 1)
                if i >= 1:
                    hidden_hi(i - 1)

        @block.vector
        def _(dve):
            count = [0]

            def step(ins):
                ins.then_inc(dch, 1)
                count[0] += 1
                return count[0]

            def need(n):
                dve.wait_ge(dch, n)

            def rstd(j, std, n):
                r = [RS[:, k, 4 * j:4 * j + 4] for k in range(6)]
                nc.vector.tensor_scalar(r[0], MV[:, 4 * j:4 * j + 4, 1], 1e-5, None, ALU.add).then_inc(var_d, 1)
                dve.wait_ge(var_d, n)
                dve.wait_ge(std, j + 1)
                need(step(nc.vector.reciprocal(r[2], r[1])))
                need(step(nc.vector.tensor_tensor(r[3], r[2], r[2], ALU.mult)))
                need(step(nc.vector.tensor_tensor(r[4], r[3], r[0], ALU.mult)))
                need(step(nc.vector.tensor_scalar(r[3], r[4], -0.5, 1.5, ALU.mult, ALU.add)))
                need(step(nc.vector.tensor_tensor(r[5], r[2], r[3], ALU.mult)))

            def normalised(j, to, done):
                for n in range(4 * j, 4 * j + 4):
                    nc.vector.tensor_scalar(to[:, n, :], XS[:, n, :], MV[:, n, 0:1], RS[:, 5, n:n + 1],
                                            ALU.subtract, ALU.mult).then_inc(done, 1)

            def layer_norm(j):
                dve.wait_ge(xin[j], 16)
                for n in range(4 * j, 4 * j + 4):
                    at = step(nc.vector.bn_stats(ST[:, n, :], XS[:, n, :]))
                for n in range(4 * j, 4 * j + 4):
                    need(at - 3 + n - 4 * j)
                    last = step(nc.vector.bn_aggr(MV[:, n, :], ST[:, n, :]))
                need(last)
                rstd(j, std_a, j + 1)
                normalised(j, XN, xn_ready)

            def rope(i):
                half, j, rows = rotated(i)
                tok = slice(j * 512, (j + 1) * 512)
                p1, p2 = 2 * (i % 2), 2 * (i % 2) + 1
                if i >= 2:
                    dve.wait_ge(roped, i - 1)
                if i >= 3:
                    dve.wait_ge(hi_a, i - 2)
                    dve.wait_ge(rem_p, i - 2)
                if half is None:
                    dve.wait_ge(k_ready, j + 1)
                    kp = PS[:, 4 + j % 2, :]
                    step(nc.vector.tensor_tensor(RT[0:64, p1, :], kp[0:64, :], COS[0:64, tok], ALU.mult))
                    need(step(nc.vector.tensor_tensor(RT[0:64, p2, :], kp[64:128, :], KSIN[64:128, tok], ALU.mult)))
                else:
                    dve.wait_ge(q_ready, j + 1)
                    qa, qb = PS[:, q_bank(j, half), :], PS[:, q_bank(j, 1 - half), :]
                    step(nc.vector.tensor_tensor(RT[:, p1, :], qa, COS[:, tok], ALU.mult))
                    need(step(nc.vector.tensor_tensor(RT[:, p2, :], qb, SIN[:, tok], ALU.mult)))
                nc.vector.tensor_tensor(RT[0:rows, 4 + i % 3, :], RT[0:rows, p1, :], RT[0:rows, p2, :],
                                        ALU.subtract if half == 0 else ALU.add).then_inc(roped, 1)

            layer_norm(0)
            dve.wait_ge(id_in, 16)
            nc.vector.tensor_copy(IDB[:], ID[:]).then_inc(idb_set, 1)
            layer_norm(1)
            dve.wait_ge(k_tab_in, 32)
            for j in range(2, NC):
                rope(j - 2)
                layer_norm(j)
            dve.wait_ge(q_tab_in, 32)
            for i in range(NC - 2, NR - 2):
                rope(i)

            def largest_v(h):
                dve.wait_ge(v_sb, NC * (h + 1))
                return nc.vector.tensor_reduce(AM[:, h:h + 1], VF[:, h * 2048:(h + 1) * 2048], AX.X, ALU.max,
                                               apply_absolute_value=True)

            step(largest_v(0))
            for i in range(NR - 2, NR):
                rope(i)

            def maximum(b, u):
                dve.wait_ge(x_ready, 16 * b + u + 1)
                if u == 0 and not (isinstance(b, int) and b == 0):
                    dve.wait_ge(nm_d, 5 * b - 4)
                nc.vector.tensor_reduce(MX[:, u // 4, u % 4:u % 4 + 1], PS[:, 4 + u % 2, :], AX.X,
                                        ALU.max).then_inc(x_read, 1)

            def split_max(b, k):
                if k == 0:
                    dve.wait_ge(x_read, 16 * b + 16)
                    ins = nc.vector.tensor_reduce(NM[:, :], MX[:, :, :], AX.X, ALU.max, negate=True)
                else:
                    dve.wait_ge(nm_d, 5 * b + k)
                    ins = (None,
                           lambda: nc.vector.tensor_copy(MP[:, :, 0], NM[:, :]),
                           lambda: nc.vector.tensor_tensor(R1[:, :], NM[:, :], MP[:, :, 0], ALU.subtract),
                           lambda: nc.vector.tensor_copy(MP[:, :, 1], R1[:, :]),
                           lambda: nc.vector.tensor_tensor(MP[:, :, 2], R1[:, :], MP[:, :, 1], ALU.subtract))[k]()
                ins.then_inc(nm_d, 1)

            def normalise(b, k):
                if k == 0:
                    dve.wait_ge(evac, b + 1)
                    nc.vector.reciprocal(RR[:, :], EV[:, :, DV]).then_inc(rr_d, 1)
                else:
                    dve.wait_ge(rr_d, b + 1)
                    dve.wait_ge(cs_p, b + 1)
                    rr = RR[:, :].rearrange("p (i o) -> p i o", o=1).to_broadcast([P, 4, DV])
                    nc.vector.scalar_tensor_tensor(
                        out=QF[:, bass.ds(b, 1), :, :].rearrange("p o i e -> p (o i) e"), in0=CS[:, :, :],
                        scalar=SC[:, 6:7], in1=rr, op0=ALU.mult, op1=ALU.mult).then_inc(norm_d, 1)

            def dve_block(b, first=False, ahead=2):
                for s in range(STEPS):
                    t = 8 * b + s
                    dve.wait_ge(e_done, t + 1)
                    if not (first and s < 4):
                        dve.wait_ge(pv_done, t - 3)
                    nc.vector.tensor_tensor(PR[:, s % 4, POOLW:], PF[:, s % 4, POOLW:], PHI[:, s % 4, POOLW:],
                                            ALU.subtract).then_inc(r_dve, 1)
                    if not first and s in (4, 5):
                        normalise(b - 1, s - 4)
                    for n, (d, u) in enumerate(max_tiles(s)):
                        if d <= ahead:
                            maximum(b + d, u)
                        if ahead >= 1 and 1 <= 2 * s + n <= 5:
                            split_max(b + 1, 2 * s + n - 1)

            def v_scale():
                dve.wait_ge(aall_p, 1)
                need(step(nc.vector.tensor_scalar(SC[:, 2:3].bitcast(u32), SC[:, 1:2].bitcast(u32), 0x7f800000, None,
                                                  ALU.bitwise_and)))
                need(step(nc.vector.tensor_scalar(SC[:, 3:4], SC[:, 2:3], 2.0 ** -100, 2.0 ** 126, ALU.max, ALU.min)))
                need(step(nc.vector.reciprocal(SC[:, 4:5], SC[:, 3:4])))
                step(nc.vector.tensor_scalar(SC[:, 6:7], SC[:, 3:4], 2.0 ** -13, None, ALU.mult))
                nc.vector.tensor_scalar(SC[:, 5:6], SC[:, 4:5], 2.0 ** 13, None, ALU.mult).then_inc(vscale, 1)

            def v_low(h):
                dve.wait_ge(vscale, 1)
                dve.wait_ge(v_hi, h + 1)
                nc.vector.scalar_tensor_tensor(
                    out=v_part(h, DV + 1), in0=v_float(h), scalar=SC[:, 5:6], in1=v_part(h, 0),
                    op0=ALU.mult, op1=ALU.subtract).then_inc(vp_ready, 1)

            for u in range(16):
                maximum(0, u)
                if u == 0:
                    need(step(largest_v(1)))
                    nc.vector.tensor_reduce(SC[:, 0:1], AM[:, :], AX.X, ALU.max).then_inc(amax_d, 1)
                if u == 3:
                    v_scale()
            for k in range(5):
                split_max(0, k)
            for h in range(2):
                v_low(h)
            for u in range(AHEAD):
                maximum(1, u)
            dve_block(0, first=True)
            with dve.Fori(1, NB - 2) as b:
                dve_block(b)
            dve_block(NB - 2, ahead=1)
            dve_block(NB - 1, ahead=0)
            for k in range(2):
                normalise(NB - 1, k)

            def ternary(i):
                raw, q = ((RW1, W1Q), (RW2, W2Q), (RW3, W3Q))[i]
                need(step(nc.vector.tensor_scalar(raw, raw, WS[:, 12 + i:13 + i], -1.0, ALU.mult, ALU.max)))
                need(step(nc.vector.tensor_scalar(raw, raw, 1.0, 12582912.0, ALU.min, ALU.add)))
                nc.vector.tensor_scalar(q.rearrange("p c n -> p (c n)"), raw, -12582912.0, None,
                                        ALU.add).then_inc(w_tern, 1)

            def norm_low(j):
                for c in range(DC):
                    dve.wait_ge(t2_hi, 2 * j + c + 1)
                    tok = slice(j * 512, (j + 1) * 512)
                    nc.vector.tensor_tensor(T2L[:, c, tok], PS[:, 6 + c, :], T2H[:, c, tok],
                                            ALU.subtract).then_inc(t2_lo, 1)

            for hp in range(2):
                context_half(dve, nc.vector.tensor_copy, ct_d, 0, 1, hp)
            for n in range(NT):
                if n % 2 == 0 and n < NT - 2:
                    for hp in range(2):
                        context_half(dve, nc.vector.tensor_copy, ct_d, n // 2 + 1, 1, hp)
                dve.wait_ge(y_ready, n + 1)
                dve.wait_ge(bo_p, n + 1)
                need(step(nc.vector.tensor_tensor(XS[:, n, :], XS[:, n, :], PS[:, 4 + n % 2, 0:D], ALU.add)))
                need(step(nc.vector.bn_stats(ST[:, n, :], XS[:, n, :])))
                nc.vector.bn_aggr(MV[:, n, :], ST[:, n, :]).then_inc(y_read, 1)
                if n == 7:
                    dve.wait_ge(wsum, 1)
                    need(step(nc.vector.tensor_scalar(WS[:, 8:11], PS[:, 4, 256:259], 1.0 / (D * FF), 1e-8,
                                                      ALU.mult, ALU.add)))
                    nc.vector.reciprocal(WS[:, 12:15], WS[:, 8:11]).then_inc(wgam, 1)
                    dve.wait_ge(wgam, 1)
                if n % 4 == 3:
                    dve.wait_ge(y_read, n + 1)
                    rstd(n // 4, std2_a, NC + n // 4 + 1)
                    normalised(n // 4, X2, x2_ready)
                if n % 4 == 1 and n >= 5:
                    norm_low(n // 4 - 1)
                if n in (10, 12, 14):
                    ternary(n // 2 - 5)
            NG = NC * len(FCH)

            def hidden_lo(i):
                j, f = divmod(i, len(FCH))
                rows = FCH[f][1]
                dve.wait_ge(hh_a, i + 1)
                nc.vector.tensor_tensor(HP[0:rows, j % 2, 1, f, :], HD[0:rows, i % 4, :], HP[0:rows, j % 2, 0, f, :],
                                        ALU.subtract).then_inc(hl_d, 1)

            def results(j):
                for i in range(4):
                    n = 4 * j + i
                    dve.wait_ge(o_ready, n + 1)
                    nc.vector.tensor_tensor(XS[:, n, :], XS[:, n, :], PS[:, 6 + n % 2, 0:D], ALU.add).then_inc(o_sb, 1)

            for i in range(NG):
                if i == 2:
                    norm_low(NC - 1)
                rows = FCH[i % len(FCH)][1]
                dve.wait_ge(sig_a, i + 1)
                if i >= 4:
                    dve.wait_ge(hl_d, i - 3)
                nc.vector.tensor_tensor(HD[0:rows, i % 4, :], SG[0:rows, i % 2, :], PS[0:rows, 2 * (i % 3) + 1, :],
                                        ALU.mult).then_inc(hid_d, 1)
                if i >= 1:
                    hidden_lo(i - 1)
                if i % len(FCH) == len(FCH) - 1 and i >= len(FCH):
                    results(i // len(FCH) - 1)
            hidden_lo(NG - 1)
            results(NC - 1)

        @block.tensor
        def _(pe):
            def q_tile(j):
                if j == 3:
                    pe.wait_ge(roped, NC + 4)
                for half in range(2):
                    for c in range(DC):
                        last = nc.tensor.matmul(PS[:, q_bank(j, half), :], WQ[:, c, P * (1 + half):P * (2 + half)],
                                                XNT[:, c, j * 512:(j + 1) * 512], start=c == 0, stop=c == DC - 1)
                last.then_inc(q_ready, 1)

            def v_tile(n):
                if n == 0:
                    pe.wait_ge(roped, NC + 2)
                if n >= 2:
                    pe.wait_ge(v_sb, n - 1)
                for i in range(2):
                    tt = 2 * n + i
                    for c in range(DC):
                        last = nc.tensor.matmul(PS[:, 6 + n % 2, i * D:(i + 1) * D], XNT[:, c, tt * P:(tt + 1) * P],
                                                WQ[:, c, 3 * P:3 * P + NKV * DV], start=c == 0, stop=c == DC - 1)
                last.then_inc(v_ready, 1)

            pe.wait_ge(id_in, 16)
            for j in range(NC):
                tok = slice(j * 512, (j + 1) * 512)
                if j >= 2:
                    pe.wait_ge(xnt_a, 2 * (j - 1))
                for i in range(4):
                    n = 4 * j + i
                    pe.wait_ge(xn_ready, n + 1)
                    for c in range(DC):
                        last = nc.tensor.transpose(PS[:, 2 * (j % 2) + c, i * P:(i + 1) * P],
                                                   XN[:, n, c * P:(c + 1) * P], ID[:])
                last.then_inc(tr_ready, 1)
                if j == 0:
                    pe.wait_ge(wq_in, 16)
                pe.wait_ge(xnt_a, 2 * (j + 1))
                if j >= 2:
                    pe.wait_ge(roped, j - 1)
                for c in range(DC):
                    last = nc.tensor.matmul(PS[:, 4 + j % 2, :], WQ[:, c, 0:P], XNT[:, c, tok],
                                            start=c == 0, stop=c == DC - 1)
                last.then_inc(k_ready, 1)
                if j == 1:
                    q_tile(0)
            for j in (1, 2):
                q_tile(j)
            for n in range(2 * NC):
                v_tile(n)
                if n == 4:
                    q_tile(3)

            def max_tile(b, u):
                i, c = divmod(u, 4)
                if not (isinstance(b, int) and b == 0 and u < 2):
                    pe.wait_ge(x_read, 16 * b + u - 1)
                nc.tensor.matmul(PS[:, 4 + u % 2, :],
                                 QC[0:KROWS, bass.ds(b, 1), i * P:(i + 1) * P].rearrange("p o n -> p (o n)"),
                                 KA[0:KROWS, bass.ds(kv_of(b) * L + c * 512, 512)],
                                 start=True, stop=True).then_inc(x_ready, 1)

            def max_transposes(b):
                pe.wait_ge(nm_d, 5 * b + 5)
                for i in range(4):
                    last = nc.tensor.transpose(MT[MROW:MROW + 4, i * P:(i + 1) * P], MP[:, i, :], IDB[:])
                last.then_inc(mt_ready, 1)

            def scores(b, s):
                for k in range(2):
                    last = nc.tensor.matmul(SCO[:, 2 * (s % 2) + k, :],
                                            KA[0:QROWS, bass.ds(kv_of(b) * L + (2 * s + k) * P, P)],
                                            QC[0:QROWS, bass.ds(b, 1), :].rearrange("p o n -> p (o n)"),
                                            start=True, stop=True)
                last.then_inc(s_ready, 1)

            def product(b, s, k):
                for i in range(4):
                    col = k * 512 + i * P
                    for w, (p, cols) in enumerate(((PHI, 129), (PR, PRW))):
                        last = nc.tensor.matmul(
                            ACC[:, i, 0:cols], p[:, s % 4, col:col + P],
                            VP[:, 2 * s + k, bass.ds(kv_of(b), 1), 0:cols].rearrange("p o e -> p (o e)"),
                            start=(s == 0 and k == 0 and i % 2 == 0 and w == 0),
                            stop=(s == STEPS - 1 and k == 1 and w == 1), skip_group_check=True)
                return last

            def tile(b, s, n, ahead):
                d, u = max_tiles(s)[n]
                if d <= ahead:
                    max_tile(b + d, u)

            def pe_block(b, first=False, ahead=2):
                for s in range(STEPS):
                    t = 8 * b + s
                    if s < STEPS - 2 or ahead >= 1:
                        pe.wait_ge(e_done, t + 1)
                        if s < STEPS - 2:
                            scores(b, s + 2)
                        else:
                            if s == STEPS - 2:
                                pe.wait_ge(m_rows, b + 2)
                            scores(b + 1, s - (STEPS - 2))
                    if s != 5:
                        tile(b, s, 0, ahead)
                    if s == 0 and not first:
                        pe.wait_ge(evac, b)
                    pe.wait_ge(r_pool, t + 1)
                    product(b, s, 0)
                    if s == 5:
                        if ahead >= 2:
                            pe.wait_ge(m_rows, b + 2)
                        tile(b, s, 0, ahead)
                    tile(b, s, 1, ahead)
                    pe.wait_ge(r_dve, t + 1)
                    product(b, s, 1).then_inc(pv_done, 1)
                    if s == 4 and ahead >= 1:
                        if ahead >= 2:
                            pe.wait_ge(x_read, 16 * (b + 2) + max_tiles(4)[0][1] + 1)
                        max_transposes(b + 1)

            pe.wait_ge(k_in, 16 * len(TERMS))
            pe.wait_ge(roped, NC)
            pe.wait_ge(q_in[0], 16 * len(TERMS))
            pe.wait_ge(k_ones, 1)
            pe.wait_ge(idb_set, 1)
            pe.wait_ge(cst_set, 2)
            for u in range(16):
                max_tile(0, u)
            pe.wait_ge(x_read, 16)
            max_transposes(0)
            pe.wait_ge(m_rows, 1)
            pe.wait_ge(roped, NR)
            pe.wait_ge(q_in[1], 16 * len(TERMS))
            for u in range(AHEAD):
                max_tile(1, u)
                if u in (0, 6):
                    scores(0, u // 6)
            pe.wait_ge(vp_ready, 2)
            pe.wait_ge(v_sb, 2 * NC)
            pe.wait_ge(q_in[2], 16 * len(TERMS))
            pe_block(0, first=True)
            pe.wait_ge(q_in[3], 16 * len(TERMS))
            pe.wait_ge(q_in[4], 16 * len(TERMS))
            with pe.Fori(1, NB - 3, 2) as b:
                pe_block(b)
                pe_block(b + 1)
            pe_block(NB - 3)
            pe_block(NB - 2, ahead=1)
            pe_block(NB - 1, ahead=0)

            def turn(m):
                if m >= 1:
                    pe.wait_ge(ct_a, 2 * m)
                    pe.wait_ge(ct_d, 2 * m)
                pe.wait_ge(norm_d, (NH - 1) * NC + m // 2 + 1)
                for h in range(NH):
                    hp, c = h % 2, h // 2
                    last = nc.tensor.transpose(
                        PS[:, 2 * hp + c // 4, (c % 4) * P:(c % 4 + 1) * P],
                        QF[:, h * NC + m // 2, 2 * (m % 2):2 * (m % 2) + 2, :].rearrange("p i e -> p (i e)"), ID[:])
                last.then_inc(ct_ready, 1)

            def project(n):
                if n % 2 == 0:
                    pe.wait_ge(ct_a, n + 2)
                    pe.wait_ge(ct_d, n + 2)
                if n >= 2:
                    pe.wait_ge(y_read, n - 1)
                for c in range(OC):
                    last = nc.tensor.matmul(PS[:, 4 + n % 2, 0:D], CT[:, n // 2 % 2, n % 2, c, :], WO[:, c, :],
                                            start=c == 0, stop=c == OC - 1)
                last.then_inc(y_ready, 1)

            def second_turn(j):
                if j >= 1:
                    pe.wait_ge(t2_lo, 2 * j)
                for c in range(DC):
                    for i in range(4):
                        pe.wait_ge(x2_ready, 4 * j + i + 1)
                        last = nc.tensor.transpose(PS[:, 6 + c, i * P:(i + 1) * P],
                                                   X2[:, 4 * j + i, c * P:(c + 1) * P], ID[:])
                    last.then_inc(t2_ready, 1)

            pe.wait_ge(e_done, 8 * NB)
            pe.wait_ge(wo_in, 16)
            turn(0)
            for m in range(NT // 2):
                if m + 1 < NT // 2:
                    turn(m + 1)
                if m == 4:
                    pe.wait_ge(wgam, 1)
                project(2 * m)
                if m % 2 == 0 and m >= 2:
                    second_turn(m // 2 - 1)
                project(2 * m + 1)
                if m == 3:
                    pe.wait_ge(ones_set, 1)
                    pe.wait_ge(wabs, 3)
                    pe.wait_ge(y_read, 7)
                    nc.tensor.matmul(PS[:, 4, 256:259], ONES[:], WS[:, 0:3], start=True, stop=True).then_inc(wsum, 1)

            def up(i):
                j, f = divmod(i, len(FCH))
                h0, rows = FCH[f]
                tok = slice(j * 512, (j + 1) * 512)
                if i >= 3:
                    pe.wait_ge(hid_d, i - 2)
                for w, wq in enumerate((W1Q, W2Q)):
                    for c in range(DC):
                        for k, part in enumerate((T2H, T2L)):
                            last = nc.tensor.matmul(PS[0:rows, 2 * (i % 3) + w, :], wq[:, c, h0:h0 + rows],
                                                    part[:, c, tok], start=(c == 0 and k == 0),
                                                    stop=(c == DC - 1 and k == 1))
                last.then_inc(g_ready, 1)

            def down(j):
                pe.wait_ge(hl_d, (j + 1) * len(FCH))
                for i in range(4):
                    n = 4 * j + i
                    if n >= 2:
                        pe.wait_ge(o_sb, n - 1)
                    for f, (_, rows) in enumerate(FCH):
                        for k in range(2):
                            last = nc.tensor.matmul(PS[:, 6 + n % 2, 0:D], HP[0:rows, j % 2, k, f, i * P:(i + 1) * P],
                                                    W3Q[0:rows, f, :], start=(f == 0 and k == 0),
                                                    stop=(f == len(FCH) - 1 and k == 1))
                    last.then_inc(o_ready, 1)

            pe.wait_ge(w_tern, 3)
            for j in range(NC):
                if j == 0:
                    pe.wait_ge(y_read, NT)
                pe.wait_ge(t2_lo, 2 * (j + 1))
                for f in range(len(FCH)):
                    up(j * len(FCH) + f)
                    if j == 0 and f == 2:
                        second_turn(NC - 1)
                if j == 1:
                    pe.wait_ge(t2_lo, 2 * NC)
                if j >= 1:
                    down(j - 1)
            down(NC - 1)


def kernel(**inputs):
    import concourse.bacc as bacc
    from concourse.bass_utils import run_bass_kernel_spmd

    def arr(name):
        return np.ascontiguousarray(inputs["L0_" + name])

    w = arr("attn_W_attn")
    qd, kd = NH * DK, NKV * DK
    qcols = np.arange(qd).reshape(NH, 2, HF)
    kcols = qd + np.arange(kd).reshape(NKV, 2, HF)
    order = np.concatenate([kcols.ravel(), kcols[:, ::-1].ravel(), qcols[:, 0].ravel(), qcols[:, 1].ravel(),
                            np.arange(qd + kd, w.shape[1])])
    inv = (np.float32(1.0) / np.float32(10000.0) ** (np.arange(0, DK, 2, dtype=np.float32) / np.float32(DK)))
    ang = inv.astype(np.float32)[:, None] * np.arange(L, dtype=np.float32)[None, :]
    half = np.float32(DK ** -0.25)
    arrays = {
        "x": arr("attn_x").reshape(L, D),
        "w_qkv": np.ascontiguousarray(w[:, order]),
        "w_out": arr("attn_W_out"),
        "b_out": arr("attn_b_out").reshape(1, D),
        "w1t": np.ascontiguousarray(arr("ffn_w1").T),
        "w2t": np.ascontiguousarray(arr("ffn_w2").T),
        "w3t": np.ascontiguousarray(arr("ffn_w3").T),
        "cos_t": np.tile(np.cos(ang) * half, (P // HF, 1)),
        "sin_t": np.tile(np.sin(ang) * half, (P // HF, 1)),
        "ksin_t": np.tile(np.concatenate([np.sin(ang) * -half, np.sin(ang) * half]), (NKV, 1)),
        "ident": np.eye(P, dtype=np.float32),
    }
    nc = bacc.Bacc("TRN2", target_bir_lowering=False, num_devices=1)
    args = [nc.dram_tensor(n + "_dram", a.shape, fp32, kind="ExternalInput").ap() for n, a in arrays.items()]
    out = nc.dram_tensor("out_dram", (L, D), fp32, kind="ExternalOutput").ap()
    layer(nc, *args, out)
    r = run_bass_kernel_spmd(nc, [{n + "_dram": a for n, a in arrays.items()}], core_ids=[0])
    return r.results[0]["out_dram"].reshape(1, L, D)
```

```python
import concourse.bass as bass
from concourse import mybir
from contextlib import ExitStack
import numpy as np

fp32 = mybir.dt.float32
bf16 = mybir.dt.bfloat16
fp16 = mybir.dt.float16
u32 = mybir.dt.uint32
ALU = mybir.AluOpType
ACT = mybir.ActivationFunctionType
AX = mybir.AxisListType

L, D = 2048, 256
NH, NKV, DK, DV = 16, 4, 16, 64
HF = DK // 2
FF = 704
P = 128
NT = L // P
NC = L // 512
DC = D // P
NB = NH * NC
STEPS = NT // 2
KROWS = 6 * DK
MROW = KROWS
QROWS = KROWS + 4
SHIFT = 8.3125
ACCW = 2 * DV + 1
VW = ACCW + 1
POOLW = 736
LASTW = 512
FCH = [(i * P, min(P, FF - i * P)) for i in range((FF + P - 1) // P)]
OC = NH * DV // P
AHEAD = 14
NR = NC * 3
PSLOTS = 6
TERMS = [(0, 0), (0, 1), (1, 0), (1, 1), (0, 2), (2, 0)]


def layer(nc, x, w_qkv, w_out, b_out, w1t, w2t, w3t, cos_t, sin_t, ksin_t, ident, out):
    q_parts = nc.dram_tensor("q_parts", (3, NH, 2, HF, L), bf16, kind="Internal").ap()
    k_parts = nc.dram_tensor("k_parts", (3, NKV * DK, L), bf16, kind="Internal").ap()

    ctx = ExitStack()
    with ctx:
        def sb(name, shape, dt):
            return ctx.enter_context(nc.sbuf_tensor(name, shape, dt))

        def sem(name):
            return ctx.enter_context(nc.semaphore(name))

        QC = sb("QC", [P, NB, 512], bf16)
        KA = sb("KA", [P, NKV * L], bf16)
        VP = sb("VP", [P, NT, NKV, VW], fp16)
        PF = sb("PF", [P, 4, 1024], fp32)
        PR = sb("PR", [P, 4, 1024], fp16)
        MX = sb("MX", [P, 4, 4], fp32)
        NM = sb("NM", [P, 4], fp32)
        R1 = sb("R1", [P, 4], fp32)
        MP = sb("MP", [P, 4, 4], bf16)
        EV = sb("EV", [P, 4, ACCW], fp32)
        CS = sb("CS", [P, 4, DV], fp32)
        RR = sb("RR", [P, 4], fp32)
        XS = sb("XS", [P, NT, D], fp32)
        WO = sb("WO", [P, 2, OC, D], fp16)
        WT = sb("WT", [P, 2 * DC * FF + len(FCH) * D], fp16)
        W1Q = WT[:, 0:DC * FF].rearrange("p (c n) -> p c n", c=DC)
        W2Q = WT[:, DC * FF:2 * DC * FF].rearrange("p (c n) -> p c n", c=DC)
        W3Q = WT[:, 2 * DC * FF:].rearrange("p (c n) -> p c n", c=len(FCH))
        PT = sb("PT", [P, PSLOTS, 3, 512], bf16)
        XNT = sb("XNT", [P, DC, L], fp32)
        ID = sb("ID", [P, P], fp32)
        IDB = sb("IDB", [P, P], bf16)
        IDH = sb("IDH", [P, P], fp16)
        ONES = sb("ONES", [P, P], fp32)
        BO = sb("BO", [P, D], fp32)
        ST = sb("ST", [P, NT, 6], fp32)
        MV = sb("MV", [P, NT, 2], fp32)
        RS = sb("RS", [P, 6, NT], fp32)
        WS = sb("WS", [P, 16], fp32)
        AM = sb("AM", [P, 2], fp32)
        YS = sb("YS", [P, 1], fp32)
        WC = sb("WC", [P, 8], fp32)
        SC = sb("SC", [P, 8], fp32)

        QCF = QC[:, :, :].rearrange("p b n -> p (b n)").bitcast(fp32)
        XN = PF[:, :, :].rearrange("p a b -> p (a b)").rearrange("p (t n) -> p t n", t=NT)
        VF = PF[:, :, :].rearrange("p a b -> p (a b)")
        COS = WO[:, :, :, :].rearrange("p w c n -> p (w c n)").bitcast(fp32)
        SIN = WT[:, 0:2 * L].bitcast(fp32)
        KSIN = QCF[:, 8192:10240]
        RT = QCF[:, 10240:15360].rearrange("p (s n) -> p s n", n=512)
        WQ = PR[:, :, :].rearrange("p a b -> p (a b)").bitcast(fp32)[:, 0:1280].rearrange("p (c n) -> p c n", c=DC)
        QF = QC[:, :, :].rearrange("p b n -> p (b n)").bitcast(fp16)\
            .rearrange("p (b w i e) -> p b w i e", b=NB, w=2, i=4)
        CT = KA[:, :].bitcast(fp16).rearrange("p (r i w c t) -> p r i w c t", r=2, i=2, w=2, c=OC)
        CTW = KA[:, :].bitcast(u32).rearrange("p (r i n) -> p r i n", r=2, i=2)
        WR = XNT[:, 1, :]
        X2 = PF[:, :, :].rearrange("p a b -> p (a b)").rearrange("p (t n) -> p t n", t=NT)
        T2H = PR[:, :, :].rearrange("p a b -> p (a b)").rearrange("p (c t) -> p c t", c=DC)
        T2L = XNT[:, 0, :].bitcast(fp16).rearrange("p (c t) -> p c t", c=DC)
        HP = QCF[:, 0:6144].bitcast(fp16).rearrange("p (r q f t) -> p r q f t", r=2, q=2, f=len(FCH))
        SG = QCF[:, 8192:9216].rearrange("p (r t) -> p r t", r=2)
        HD = QCF[:, 9216:11264].rearrange("p (r t) -> p r t", r=4)
        PHI = PF[:, :, :].rearrange("p a b -> p (a b)").bitcast(bf16)\
            .rearrange("p (a b two) -> p a b two", a=4, two=2)[:, :, :, 1]
        PTF = PT[:, :, :, :].rearrange("p a b c -> p (a b c)").bitcast(fp32)
        RW1, RW2, RW3 = PTF[:, 0:DC * FF], PTF[:, DC * FF:2 * DC * FF], \
            PTF[:, 2 * DC * FF:2 * DC * FF + len(FCH) * D]

        PS = ctx.enter_context(nc.psum_tensor("PS", [P, 8, 512], fp32))
        SCO = PS[:, 0:4, :]
        ACC = PS[:, 6:8, :].rearrange("p b (i n) -> p (b i) n", i=2)[:, :, 0:ACCW]
        MT = PS[:, 4, :].bitcast(bf16)

        xin = [sem(f"xin{j}") for j in range(NC)]
        (wq_in, k_tab_in, q_tab_in, id_in, bo_in, wo_in) = map(sem, (
            "wq_in", "k_tab_in", "q_tab_in", "id_in", "bo_in", "wo_in"))
        rw_in = [sem(f"rw_in{i}") for i in range(3)]
        (ones_set, idb_set, cst_set) = map(sem, ("ones_set", "idb_set", "cst_set"))
        dch = sem("dch")
        (std_a, xn_ready, tr_ready, xnt_a, rw_zero) = map(sem, ("std_a", "xn_ready", "tr_ready", "xnt_a", "rw_zero"))
        (k_ready, q_ready, v_ready, v_sb, roped, hi_a, rem_p, mid_a, low_p) = map(sem, (
            "k_ready", "q_ready", "v_ready", "v_sb", "roped", "hi_a", "rem_p", "mid_a", "low_p"))
        parts_out = [sem(f"parts_out{i}") for i in range(PSLOTS)]
        q_in = [sem(f"q_in{j}") for j in range(NC + 1)]
        v_scaled = sem("v_scaled")
        (k_in, k_ones, amax_d, aall_p, vscale, v_hi, vp_ready) = map(sem, (
            "k_in", "k_ones", "amax_d", "aall_p", "vscale", "v_hi", "vp_ready"))
        (wabs, wsum, wgam, w_tern) = map(sem, ("wabs", "wsum", "wgam", "w_tern"))
        s_ready = sem("s_ready")
        e_done = sem("e_done")
        x_ready = sem("x_ready")
        x_read = sem("x_read")
        nm_d = sem("nm_d")
        mt_ready = sem("mt_ready")
        m_rows = sem("m_rows")
        r_pool = sem("r_pool")
        r_dve = sem("r_dve")
        pv_done = sem("pv_done")
        evac = sem("evac")
        rr_d = sem("rr_d")
        cs_p = sem("cs_p")
        norm_d = sem("norm_d")
        (var_d, bo_p) = map(sem, ("var_d", "bo_p"))
        ctx_hi = sem("ctx_hi")
        ctx_lo = sem("ctx_lo")
        (wo_amax, wo_all, wo_scale, wo_hi, wo_lo) = map(sem, ("wo_amax", "wo_all", "wo_scale", "wo_hi", "wo_lo"))
        (ct_ready, ct_a, ct_d, y_ready, y_read, t2_ready, t2_hi, t2_lo) = map(sem, (
            "ct_ready", "ct_a", "ct_d", "y_ready", "y_read", "t2_ready", "t2_hi", "t2_lo"))
        (x2_ready, std2_a, g_ready, sig_a, hid_d, hh_a, hl_d, o_ready, o_sb, o_out) = map(sem, (
            "x2_ready", "std2_a", "g_ready", "sig_a", "hid_d", "hh_a", "hl_d", "o_ready", "o_sb", "o_out"))
        block = ctx.enter_context(nc.Block())

        def kv_of(b):
            return b // (NB // NKV)

        def max_tiles(s):
            return [(1 if s < 1 else 2, (2 * s + AHEAD) % 16 + n) for n in range(2)]

        def rotated(i):
            return (None, i, 64) if i < NC else ((i - NC) % 2, (i - NC) // 2, P)

        def q_bank(j, half):
            return (6, 0, 2, 0)[j] + half

        def sent(i):
            before = [16 * (1 if n < NC else 3) for n in range(i % PSLOTS, i + 1, PSLOTS)]
            return parts_out[i % PSLOTS], sum(before)

        def v_part(h, at):
            return VP[:, h * NT // 2:(h + 1) * NT // 2, :, at:at + DV].rearrange("p t k e -> p (t k) e")

        def v_float(h):
            return VF[:, h * 2048:(h + 1) * 2048].rearrange("p (a e) -> p a e", e=DV)

        def context_half(eng, copy, done, words, m, i, hp):
            eng.wait_ge(ct_ready, m + 1)
            if m >= 2 and hp == 0:
                eng.wait_ge(y_ready, 2 * (m - 1))
            rows, banks = slice(64 * hp, 64 * hp + 64), PS[64 * i:64 * i + 64, 2 * hp:2 * hp + 2, :]
            if words:
                copy(CTW[rows, m % 2, i, :], banks.rearrange("p b n -> p (b n)").bitcast(u32)).then_inc(done, 1)
            else:
                copy(CT[rows, m % 2, i, :, :, :].rearrange("p w c t -> p (w c t)"),
                     banks.rearrange("p b n -> p (b n)").bitcast(fp16)).then_inc(done, 1)

        @block.sync
        def _(sp):
            for j in range(NC):
                sp.dma_start(XS[:, 4 * j:4 * j + 4, :],
                             x[j * 512:(j + 1) * 512, :].rearrange("(t p) d -> p t d", p=P)).then_inc(xin[j], 16)
                if j == 0:
                    sp.dma_start(ID[:], ident).then_inc(id_in, 16)
                    sp.dma_start(WQ, w_qkv.rearrange("(c p) n -> p c n", p=P)).then_inc(wq_in, 16)
                if j == 1:
                    sp.dma_start(COS[0:64, :], cos_t[0:64, :]).then_inc(k_tab_in, 16)
                    sp.dma_start(KSIN[64:128, :], ksin_t).then_inc(k_tab_in, 16)
            sp.dma_start(COS[64:128, :], cos_t[64:128, :]).then_inc(q_tab_in, 16)
            sp.dma_start(SIN, sin_t).then_inc(q_tab_in, 16)
            sp.dma_start(BO[:], b_out.partition_broadcast(P)).then_inc(bo_in, 16)

            def send(i):
                half, j, _ = rotated(i)
                tok = slice(j * 512, (j + 1) * 512)
                sp.wait_ge(low_p, i + 1)
                if half is None:
                    sp.dma_start(k_parts[:, :, tok].rearrange("q r n -> r q n"), PT[0:64, i % PSLOTS, :, :]
                                 ).then_inc(parts_out[i % PSLOTS], 16)
                else:
                    for q in range(3):
                        sp.dma_start(q_parts[q, :, half, :, tok], PT[:, i % PSLOTS, q, :]
                                     ).then_inc(parts_out[i % PSLOTS], 16)

            def rows_of(g):
                return slice(DK * g, DK * (g + 1))

            for i in range(NC + 2):
                send(i)
            for i in range(NC):
                sp.wait_ge(*sent(i))
            for g, (_, kp) in enumerate(TERMS):
                sp.dma_start(KA[rows_of(g), :].rearrange("r (k t) -> r k t", k=NKV),
                             k_parts[kp].rearrange("(k r) t -> r k t", k=NKV)).then_inc(k_in, 16)
            heads = NH // 2
            for j in range(NC):
                for i in (NC + 2 * j, NC + 2 * j + 1):
                    if j >= 1:
                        send(i)
                for i in (NC + 2 * j, NC + 2 * j + 1):
                    sp.wait_ge(*sent(i))
                for g, (qp, _) in enumerate(TERMS):
                    sp.dma_start(QC[rows_of(g), j:heads * NC:NC, :],
                                 q_parts[qp, 0:heads, :, :, j * 512:(j + 1) * 512]
                                 .rearrange("a h f t -> (h f) a t")).then_inc(q_in[j], 16)
            for g, (qp, _) in enumerate(TERMS):
                sp.dma_start(QC[rows_of(g), heads * NC:, :].rearrange("r (a b) n -> r a (b n)", a=heads),
                             q_parts[qp, heads:].rearrange("a h f t -> (h f) a t")).then_inc(q_in[NC], 16)
            sp.wait_ge(v_ready, 2 * NC)
            sp.wait_ge(q_ready, NC)
            sp.dma_start(WR.rearrange("p (c n) -> p c n", c=OC),
                         w_out.rearrange("(c p) n -> p c n", p=P)).then_inc(wo_in, 16)
            sp.dma_start(RW1.rearrange("p (c n) -> p c n", c=DC),
                         w1t.rearrange("(c p) n -> p c n", p=P)).then_inc(rw_in[0], 16)
            sp.dma_start(RW2.rearrange("p (c n) -> p c n", c=DC),
                         w2t.rearrange("(c p) n -> p c n", p=P)).then_inc(rw_in[1], 16)
            nf = FF // P
            sp.dma_start(RW3[:, 0:nf * D].rearrange("p (c n) -> p c n", c=nf),
                         w3t[0:nf * P, :].rearrange("(c p) n -> p c n", p=P)).then_inc(rw_in[2], 16)
            sp.dma_start(RW3[0:FF - nf * P, nf * D:], w3t[nf * P:, :]).then_inc(rw_in[2], 16)
            for n in range(NT):
                sp.wait_ge(o_sb, n + 1)
                sp.dma_start(out[n * P:(n + 1) * P, :], XS[:, n, :]).then_inc(o_out, 16)
            sp.wait_ge(o_out, 16 * NT)

        @block.gpsimd
        def _(pool):
            nc.gpsimd.memset(KA[MROW:MROW + 4, :], 1.0).then_inc(k_ones, 1)
            pool.wait_ge(k_ones, 1)
            nc.gpsimd.memset(ONES[:], 1.0).then_inc(ones_set, 1)
            nc.gpsimd.memset(VP[:, :, :, DV:DV + 1], 1.0).then_inc(cst_set, 1)
            nc.gpsimd.memset(MP[:, :, 3:4], SHIFT).then_inc(cst_set, 1)
            pool.wait_ge(cst_set, 2)

            def remainder(i):
                _, _, rows = rotated(i)
                pool.wait_ge(hi_a, i + 1)
                if i >= 3:
                    pool.wait_ge(low_p, i - 2)
                nc.gpsimd.tensor_tensor(RT[0:rows, 7 + i % 3, :], RT[0:rows, 4 + i % 3, :],
                                        PT[0:rows, i % PSLOTS, 0, :], ALU.subtract).then_inc(rem_p, 1)

            def low(i):
                _, _, rows = rotated(i)
                pool.wait_ge(mid_a, i + 1)
                nc.gpsimd.tensor_tensor(PT[0:rows, i % PSLOTS, 2, :], RT[0:rows, 7 + i % 3, :],
                                        PT[0:rows, i % PSLOTS, 1, :], ALU.subtract).then_inc(low_p, 1)

            for i in range(NR + 1):
                if i < NR:
                    remainder(i)
                if i >= 1:
                    low(i - 1)
            pool.wait_ge(amax_d, 1)
            nc.gpsimd.partition_all_reduce(SC[:, 1:2], SC[:, 0:1], P, bass.bass_isa.ReduceOp.max).then_inc(aall_p, 1)
            pool.wait_ge(aall_p, 1)
            for h in range(2):
                pool.wait_ge(v_hi, h + 1)
                nc.gpsimd.tensor_tensor(v_part(h, DV + 1), v_float(h), v_part(h, 0), ALU.subtract).then_inc(vp_ready, 1)
                pool.wait_ge(vp_ready, h + 1)
            for i in range(NR - PSLOTS, NR):
                pool.wait_ge(*sent(i))
            nc.gpsimd.memset(RW3[64:128, (FF // P) * D:], 0.0).then_inc(rw_zero, 1)
            pool.wait_ge(rw_zero, 1)

            def pool_block(b, first=False, width=POOLW):
                for s in range(STEPS):
                    t = 8 * b + s
                    pool.wait_ge(e_done, t + 1)
                    if not (first and s < 4):
                        pool.wait_ge(pv_done, t - 3)
                    nc.gpsimd.tensor_tensor(PR[:, s % 4, 0:width], PF[:, s % 4, 0:width], PHI[:, s % 4, 0:width],
                                            ALU.subtract).then_inc(r_pool, 1)
                    if s == 3 and not first:
                        add_parts(b - 1)

            def add_parts(b):
                pool.wait_ge(evac, b + 1)
                nc.gpsimd.tensor_tensor(CS[:, :, :], EV[:, :, 0:DV], EV[:, :, DV + 1:ACCW], ALU.add).then_inc(cs_p, 1)

            pool_block(0, first=True)
            with pool.Fori(1, NB - 2) as b:
                pool_block(b)
            pool_block(NB - 2, width=LASTW)
            pool.wait_ge(wo_amax, 1)
            nc.gpsimd.partition_all_reduce(WC[:, 1:2], WC[:, 0:1], P, bass.bass_isa.ReduceOp.max).then_inc(wo_all, 1)
            pool_block(NB - 1, width=LASTW)
            pool.wait_ge(ctx_lo, NB - 1)
            add_parts(NB - 1)
            pool.wait_ge(bo_in, 16)
            for n in range(NT):
                nc.gpsimd.tensor_tensor(XS[:, n, :], XS[:, n, :], BO[:, :], ALU.add).then_inc(bo_p, 1)

        @block.scalar
        def _(act):
            def hi(i):
                _, _, rows = rotated(i)
                act.wait_ge(roped, i + 1)
                if i >= PSLOTS:
                    act.wait_ge(*sent(i - PSLOTS))
                nc.scalar.copy(PT[0:rows, i % PSLOTS, 0, :], RT[0:rows, 4 + i % 3, :]).then_inc(hi_a, 1)

            def mid(i):
                _, _, rows = rotated(i)
                act.wait_ge(rem_p, i + 1)
                nc.scalar.copy(PT[0:rows, i % PSLOTS, 1, :], RT[0:rows, 7 + i % 3, :]).then_inc(mid_a, 1)

            def v_out(n):
                act.wait_ge(v_ready, n + 1)
                nc.scalar.copy(VF[:, n * 512:(n + 1) * 512], PS[:, 6 + n % 2, :]).then_inc(v_sb, 1)

            def v_high(h):
                act.wait_ge(vscale, 1)
                nc.scalar.activation(v_float(h), v_float(h), ACT.Copy, scale=SC[:, 5:6]).then_inc(v_scaled, 1)
                act.wait_ge(v_scaled, h + 1)
                nc.scalar.copy(v_part(h, 0), v_float(h)).then_inc(v_hi, 1)

            def square_root(j, done):
                act.wait_ge(var_d, len(sqrts) + 1)
                nc.scalar.activation(RS[:, 1, 4 * j:4 * j + 4], RS[:, 0, 4 * j:4 * j + 4], ACT.Sqrt).then_inc(done, 1)
                sqrts.append(j)

            sqrts = []
            for j in range(NC):
                square_root(j, std_a)
                act.wait_ge(tr_ready, j + 1)
                for c in range(DC):
                    nc.scalar.copy(XNT[:, c, j * 512:(j + 1) * 512], PS[:, 2 * (j % 2) + c, :]).then_inc(xnt_a, 1)
                if j >= 1:
                    hi(j - 1)
                if j >= 2:
                    mid(j - 2)
            hi(NC - 1)
            mid(NC - 2)
            for i in range(NC, NR):
                hi(i)
                mid(i - 1)
                for n in {6: (0,), 7: (1,), 8: (2,), 9: (3, 4, 5), 11: (6, 7)}.get(i, ()):
                    v_out(n)
            mid(NR - 1)

            def take_out(b):
                act.wait_ge(pv_done, 8 * b + 8)
                nc.scalar.copy(EV[:, :, :], ACC[:, :, :]).then_inc(evac, 1)

            def max_rows(b):
                act.wait_ge(mt_ready, b + 1)
                nc.scalar.copy(QC[MROW:MROW + 4, bass.ds(b, 1), :].rearrange("p o n -> p (o n)"),
                               MT[MROW:MROW + 4, 0:512]).then_inc(m_rows, 1)

            def context_high(b):
                act.wait_ge(norm_d, b + 1)
                nc.scalar.copy(QF[:, bass.ds(b, 1), 0, :, :].rearrange("p o i e -> p (o i) e"),
                               CS[:, :, :]).then_inc(ctx_hi, 1)

            w_abs = (W1Q, W2Q, W3Q)

            def sum_abs(m):
                act.wait_ge(rw_in[m], 16 if m < 2 else 32)
                if m == 2:
                    act.wait_ge(rw_zero, 1)
                nc.scalar.activation(w_abs[m].rearrange("p c n -> p (c n)").bitcast(bf16), (RW1, RW2, RW3)[m],
                                     ACT.Abs, accum_out=WS[:, m:m + 1]).then_inc(wabs, 1)

            def act_block(b, first=False, ahead=2, sums=False):
                for s in range(STEPS):
                    t = 8 * b + s
                    act.wait_ge(s_ready, t + 1)
                    if first and s in (0, 2):
                        act.wait_ge(vp_ready, 1 + s // 2)
                    if not (first and s < 4):
                        act.wait_ge(pv_done, t - 3)
                    nc.scalar.activation(PF[:, s % 4, :].rearrange("p (k n) -> p k n", k=2),
                                         SCO[:, 2 * (s % 2):2 * (s % 2) + 2, :], ACT.Exp).then_inc(e_done, 1)
                    if s == 1 and not first:
                        take_out(b - 1)
                    if s == 6 and ahead >= 1:
                        max_rows(b + 1)
                    if s == 7 and not first:
                        context_high(b - 1)
                    if sums and s in (3, 4, 5):
                        sum_abs(s - 3)
                    if s == 4 and ahead == 0:
                        act.wait_ge(wo_scale, 1)
                        nc.scalar.activation(WO[:, 0, :, :].rearrange("p c n -> p (c n)"), WR, ACT.Copy,
                                             scale=WC[:, 5:6]).then_inc(wo_hi, 1)

            for h in range(2):
                v_high(h)
            nc.scalar.activation(WS[:, 15:16], SC[:, 5:6], ACT.Exp, scale=0.0)
            max_rows(0)
            act_block(0, first=True)
            with act.Fori(1, NB - 3) as b:
                act_block(b)
            act_block(NB - 3, sums=True)
            act_block(NB - 2, ahead=1)
            act_block(NB - 1, ahead=0)
            take_out(NB - 1)

            def norm_high(j):
                for c in range(DC):
                    act.wait_ge(t2_ready, 2 * j + c + 1)
                    nc.scalar.copy(T2H[:, c, j * 512:(j + 1) * 512], PS[:, 6 + c, :]).then_inc(t2_hi, 1)

            for m in range(NT // 2):
                for hp in range(2):
                    context_half(act, nc.scalar.copy, ct_a, False, m, 1, hp)
                if m == 0:
                    context_high(NB - 1)
                if m % 2 == 0 and m >= 2:
                    square_root(m // 2 - 1, std2_a)
                if m % 2 == 1 and m >= 3:
                    norm_high(m // 2 - 1)
            square_root(NC - 1, std2_a)
            def hidden_hi(i):
                j, f = divmod(i, len(FCH))
                act.wait_ge(hid_d, i + 1)
                if j >= 2:
                    act.wait_ge(o_ready, 4 * (j - 1))
                rows = FCH[f][1]
                nc.scalar.copy(HP[0:rows, j % 2, 0, f, :], HD[0:rows, i % 4, :]).then_inc(hh_a, 1)

            NG = NC * len(FCH)
            for i in range(NG + 1):
                if i == 2:
                    norm_high(NC - 1)
                if i < NG:
                    rows = FCH[i % len(FCH)][1]
                    act.wait_ge(g_ready, i + 1)
                    if i >= 2:
                        act.wait_ge(hid_d, i - 1)
                    nc.scalar.activation(SG[0:rows, i % 2, :], PS[0:rows, 2 * (i % 3), :],
                                         ACT.Sigmoid).then_inc(sig_a, 1)
                if i >= 1:
                    hidden_hi(i - 1)

        @block.vector
        def _(dve):
            count = [0]

            def step(ins):
                ins.then_inc(dch, 1)
                count[0] += 1
                return count[0]

            def need(n):
                dve.wait_ge(dch, n)

            def rstd(j, std, n):
                r = [RS[:, k, 4 * j:4 * j + 4] for k in range(6)]
                nc.vector.tensor_scalar(r[0], MV[:, 4 * j:4 * j + 4, 1], 1e-5, None, ALU.add).then_inc(var_d, 1)
                dve.wait_ge(var_d, n)
                dve.wait_ge(std, j + 1)
                need(step(nc.vector.reciprocal(r[2], r[1])))
                need(step(nc.vector.tensor_tensor(r[3], r[2], r[2], ALU.mult)))
                need(step(nc.vector.tensor_tensor(r[4], r[3], r[0], ALU.mult)))
                need(step(nc.vector.tensor_scalar(r[3], r[4], -0.5, 1.5, ALU.mult, ALU.add)))
                need(step(nc.vector.tensor_tensor(r[5], r[2], r[3], ALU.mult)))

            def normalised(j, to, done):
                for n in range(4 * j, 4 * j + 4):
                    nc.vector.tensor_scalar(to[:, n, :], XS[:, n, :], MV[:, n, 0:1], RS[:, 5, n:n + 1],
                                            ALU.subtract, ALU.mult).then_inc(done, 1)

            def layer_norm(j):
                dve.wait_ge(xin[j], 16)
                for n in range(4 * j, 4 * j + 4):
                    at = step(nc.vector.bn_stats(ST[:, n, :], XS[:, n, :]))
                for n in range(4 * j, 4 * j + 4):
                    need(at - 3 + n - 4 * j)
                    last = step(nc.vector.bn_aggr(MV[:, n, :], ST[:, n, :]))
                need(last)
                rstd(j, std_a, j + 1)
                normalised(j, XN, xn_ready)

            def rope(i):
                half, j, rows = rotated(i)
                tok = slice(j * 512, (j + 1) * 512)
                p1, p2 = 2 * (i % 2), 2 * (i % 2) + 1
                if i >= 2:
                    dve.wait_ge(roped, i - 1)
                if i >= 3:
                    dve.wait_ge(hi_a, i - 2)
                    dve.wait_ge(rem_p, i - 2)
                if half is None:
                    dve.wait_ge(k_ready, j + 1)
                    kp = PS[:, 4 + j % 2, :]
                    step(nc.vector.tensor_tensor(RT[0:64, p1, :], kp[0:64, :], COS[0:64, tok], ALU.mult))
                    need(step(nc.vector.tensor_tensor(RT[0:64, p2, :], kp[64:128, :], KSIN[64:128, tok], ALU.mult)))
                else:
                    dve.wait_ge(q_ready, j + 1)
                    qa, qb = PS[:, q_bank(j, half), :], PS[:, q_bank(j, 1 - half), :]
                    step(nc.vector.tensor_tensor(RT[:, p1, :], qa, COS[:, tok], ALU.mult))
                    need(step(nc.vector.tensor_tensor(RT[:, p2, :], qb, SIN[:, tok], ALU.mult)))
                nc.vector.tensor_tensor(RT[0:rows, 4 + i % 3, :], RT[0:rows, p1, :], RT[0:rows, p2, :],
                                        ALU.subtract if half == 0 else ALU.add).then_inc(roped, 1)

            layer_norm(0)
            dve.wait_ge(id_in, 16)
            nc.vector.tensor_copy(IDB[:], ID[:]).then_inc(idb_set, 1)
            nc.vector.tensor_copy(IDH[:], ID[:]).then_inc(idb_set, 1)
            layer_norm(1)
            dve.wait_ge(k_tab_in, 32)
            for j in range(2, NC):
                rope(j - 2)
                layer_norm(j)
            dve.wait_ge(q_tab_in, 32)
            for i in range(NC - 2, NR - 2):
                rope(i)

            def largest_v(h):
                dve.wait_ge(v_sb, NC * (h + 1))
                return nc.vector.tensor_reduce(AM[:, h:h + 1], VF[:, h * 2048:(h + 1) * 2048], AX.X, ALU.max,
                                               apply_absolute_value=True)

            step(largest_v(0))
            for i in range(NR - 2, NR):
                rope(i)

            def maximum(b, u):
                dve.wait_ge(x_ready, 16 * b + u + 1)
                if u == 0 and not (isinstance(b, int) and b == 0):
                    dve.wait_ge(nm_d, 5 * b - 4)
                nc.vector.tensor_reduce(MX[:, u // 4, u % 4:u % 4 + 1], PS[:, 4 + u % 2, :], AX.X,
                                        ALU.max).then_inc(x_read, 1)

            def split_max(b, k):
                if k == 0:
                    dve.wait_ge(x_read, 16 * b + 16)
                    ins = nc.vector.tensor_reduce(NM[:, :], MX[:, :, :], AX.X, ALU.max, negate=True)
                else:
                    dve.wait_ge(nm_d, 5 * b + k)
                    ins = (None,
                           lambda: nc.vector.tensor_copy(MP[:, :, 0], NM[:, :]),
                           lambda: nc.vector.tensor_tensor(R1[:, :], NM[:, :], MP[:, :, 0], ALU.subtract),
                           lambda: nc.vector.tensor_copy(MP[:, :, 1], R1[:, :]),
                           lambda: nc.vector.tensor_tensor(MP[:, :, 2], R1[:, :], MP[:, :, 1], ALU.subtract))[k]()
                ins.then_inc(nm_d, 1)

            def normalise(b, k):
                if k == 0:
                    dve.wait_ge(evac, b + 1)
                    nc.vector.reciprocal(RR[:, :], EV[:, :, DV]).then_inc(rr_d, 1)
                else:
                    dve.wait_ge(rr_d, b + 1)
                    dve.wait_ge(cs_p, b + 1)
                    rr = RR[:, :].rearrange("p (i o) -> p i o", o=1).to_broadcast([P, 4, DV])
                    nc.vector.tensor_tensor(CS[:, :, :], CS[:, :, :], rr, ALU.mult).then_inc(norm_d, 1)

            def context_low(b):
                dve.wait_ge(ctx_hi, b + 1)
                at = QF[:, bass.ds(b, 1), :, :, :]
                nc.vector.tensor_tensor(at[:, :, 1, :, :].rearrange("p o i e -> p (o i) e"), CS[:, :, :],
                                        at[:, :, 0, :, :].rearrange("p o i e -> p (o i) e"),
                                        ALU.subtract).then_inc(ctx_lo, 1)

            def ternary(i, k):
                raw, q = ((RW1, W1Q), (RW2, W2Q), (RW3, W3Q))[i]
                if k == 0:
                    need(step(nc.vector.tensor_scalar(raw, raw, WS[:, 12 + i:13 + i], -1.0, ALU.mult, ALU.max)))
                elif k == 1:
                    need(step(nc.vector.tensor_scalar(raw, raw, 1.0, 12582912.0, ALU.min, ALU.add)))
                else:
                    nc.vector.tensor_scalar(q.rearrange("p c n -> p (c n)"), raw, -12582912.0, None,
                                            ALU.add).then_inc(w_tern, 1)

            def weights(at):
                if at == 2:
                    dve.wait_ge(wsum, 1)
                    need(step(nc.vector.tensor_scalar(WS[:, 8:11], PS[:, 4, 256:259], 1.0 / (D * FF), 1e-8,
                                                      ALU.mult, ALU.add)))
                    nc.vector.reciprocal(WS[:, 12:15], WS[:, 8:11]).then_inc(wgam, 1)
                    dve.wait_ge(wgam, 1)
                if at in (4, 5):
                    dve.wait_ge(wo_in, 16)
                    need(step(nc.vector.tensor_reduce(AM[:, at - 4:at - 3], WR[:, (at - 4) * 1024:(at - 3) * 1024], AX.X,
                                                      ALU.max, apply_absolute_value=True)))
                if at == 5:
                    nc.vector.tensor_reduce(WC[:, 0:1], AM[:, :], AX.X, ALU.max).then_inc(wo_amax, 1)
                if at in (6, 7, 8):
                    ternary(0, at - 6)
                if at == 9:
                    dve.wait_ge(wo_all, 1)
                    power_of_two(WC, wo_scale)
                    dve.wait_ge(dch, count[0])
                    nc.vector.tensor_tensor(YS[:, :], WC[:, 6:7], SC[:, 6:7], ALU.mult).then_inc(wo_scale, 1)
                if at in (10, 11, 12):
                    ternary(1, at - 10)
                if at in (13, 14):
                    h = slice((at - 13) * OC // 2, (at - 12) * OC // 2)
                    dve.wait_ge(wo_hi, 1)
                    nc.vector.scalar_tensor_tensor(
                        out=WO[:, 1, h, :], in0=WR.rearrange("p (c n) -> p c n", c=OC)[:, h, :], scalar=WC[:, 5:6],
                        in1=WO[:, 0, h, :], op0=ALU.mult, op1=ALU.subtract).then_inc(wo_lo, 1)

            def dve_block(b, first=False, ahead=2):
                width = POOLW if ahead >= 2 else LASTW
                for s in range(STEPS):
                    t = 8 * b + s
                    dve.wait_ge(e_done, t + 1)
                    if not (first and s < 4):
                        dve.wait_ge(pv_done, t - 3)
                    nc.vector.tensor_tensor(PR[:, s % 4, width:], PF[:, s % 4, width:], PHI[:, s % 4, width:],
                                            ALU.subtract).then_inc(r_dve, 1)
                    if not first and s in (4, 5):
                        normalise(b - 1, s - 4)
                    for n, (d, u) in enumerate(max_tiles(s)):
                        if d <= ahead:
                            maximum(b + d, u)
                        if ahead >= 1 and 1 <= 2 * s + n <= 5:
                            split_max(b + 1, 2 * s + n - 1)
                    if s == STEPS - 1 and not first:
                        context_low(b - 1)
                    if ahead < 2:
                        weights(8 * (1 - ahead) + s)

            def power_of_two(c, done):
                need(step(nc.vector.tensor_scalar(c[:, 2:3].bitcast(u32), c[:, 1:2].bitcast(u32), 0x7f800000, None,
                                                  ALU.bitwise_and)))
                need(step(nc.vector.tensor_scalar(c[:, 3:4], c[:, 2:3], 2.0 ** -100, 2.0 ** 126, ALU.max, ALU.min)))
                need(step(nc.vector.reciprocal(c[:, 4:5], c[:, 3:4])))
                step(nc.vector.tensor_scalar(c[:, 6:7], c[:, 3:4], 2.0 ** -13, None, ALU.mult))
                nc.vector.tensor_scalar(c[:, 5:6], c[:, 4:5], 2.0 ** 13, None, ALU.mult).then_inc(done, 1)

            for u in range(16):
                maximum(0, u)
                if u == 0:
                    need(step(largest_v(1)))
                    nc.vector.tensor_reduce(SC[:, 0:1], AM[:, :], AX.X, ALU.max).then_inc(amax_d, 1)
                if u == 3:
                    dve.wait_ge(aall_p, 1)
                    power_of_two(SC, vscale)
            for k in range(5):
                split_max(0, k)
            for u in range(AHEAD):
                maximum(1, u)
            dve_block(0, first=True)
            with dve.Fori(1, NB - 2) as b:
                dve_block(b)
            dve_block(NB - 2, ahead=1)
            dve_block(NB - 1, ahead=0)
            dve.wait_ge(wo_scale, 2)

            def norm_low(j):
                for c in range(DC):
                    dve.wait_ge(t2_hi, 2 * j + c + 1)
                    tok = slice(j * 512, (j + 1) * 512)
                    nc.vector.tensor_tensor(T2L[:, c, tok], PS[:, 6 + c, :], T2H[:, c, tok],
                                            ALU.subtract).then_inc(t2_lo, 1)

            for hp in range(2):
                context_half(dve, nc.vector.tensor_copy, ct_d, True, 0, 0, hp)
            for k in range(2):
                normalise(NB - 1, k)
            context_low(NB - 1)
            for n in range(NT):
                if n % 2 == 0 and n < NT - 2:
                    for hp in range(2):
                        context_half(dve, nc.vector.tensor_copy, ct_d, True, n // 2 + 1, 0, hp)
                dve.wait_ge(y_ready, n + 1)
                dve.wait_ge(bo_p, n + 1)
                need(step(nc.vector.scalar_tensor_tensor(
                    out=XS[:, n, :], in0=PS[:, 4 + n % 2, 0:D], scalar=YS[:, 0:1], in1=XS[:, n, :],
                    op0=ALU.mult, op1=ALU.add)))
                need(step(nc.vector.bn_stats(ST[:, n, :], XS[:, n, :])))
                nc.vector.bn_aggr(MV[:, n, :], ST[:, n, :]).then_inc(y_read, 1)
                if n % 4 == 3:
                    dve.wait_ge(y_read, n + 1)
                    rstd(n // 4, std2_a, NC + n // 4 + 1)
                    normalised(n // 4, X2, x2_ready)
                if n % 4 == 1 and n >= 5:
                    norm_low(n // 4 - 1)
                if n == 10:
                    for k in range(3):
                        ternary(2, k)
            NG = NC * len(FCH)

            def hidden_lo(i):
                j, f = divmod(i, len(FCH))
                rows = FCH[f][1]
                dve.wait_ge(hh_a, i + 1)
                nc.vector.tensor_tensor(HP[0:rows, j % 2, 1, f, :], HD[0:rows, i % 4, :], HP[0:rows, j % 2, 0, f, :],
                                        ALU.subtract).then_inc(hl_d, 1)

            def results(j):
                for i in range(4):
                    n = 4 * j + i
                    dve.wait_ge(o_ready, n + 1)
                    nc.vector.tensor_tensor(XS[:, n, :], XS[:, n, :], PS[:, 6 + n % 2, 0:D], ALU.add).then_inc(o_sb, 1)

            for i in range(NG):
                if i == 2:
                    norm_low(NC - 1)
                rows = FCH[i % len(FCH)][1]
                dve.wait_ge(sig_a, i + 1)
                if i >= 4:
                    dve.wait_ge(hl_d, i - 3)
                nc.vector.tensor_tensor(HD[0:rows, i % 4, :], SG[0:rows, i % 2, :], PS[0:rows, 2 * (i % 3) + 1, :],
                                        ALU.mult).then_inc(hid_d, 1)
                if i >= 1:
                    hidden_lo(i - 1)
                if i % len(FCH) == len(FCH) - 1 and i >= len(FCH):
                    results(i // len(FCH) - 1)
            hidden_lo(NG - 1)
            results(NC - 1)

        @block.tensor
        def _(pe):
            def q_tile(j):
                if j == 3:
                    pe.wait_ge(roped, NC + 4)
                for half in range(2):
                    for c in range(DC):
                        last = nc.tensor.matmul(PS[:, q_bank(j, half), :], WQ[:, c, P * (1 + half):P * (2 + half)],
                                                XNT[:, c, j * 512:(j + 1) * 512], start=c == 0, stop=c == DC - 1)
                last.then_inc(q_ready, 1)

            def v_tile(n):
                if n == 0:
                    pe.wait_ge(roped, NC + 2)
                if n >= 2:
                    pe.wait_ge(v_sb, n - 1)
                for i in range(2):
                    tt = 2 * n + i
                    for c in range(DC):
                        last = nc.tensor.matmul(PS[:, 6 + n % 2, i * D:(i + 1) * D], XNT[:, c, tt * P:(tt + 1) * P],
                                                WQ[:, c, 3 * P:3 * P + NKV * DV], start=c == 0, stop=c == DC - 1)
                last.then_inc(v_ready, 1)

            pe.wait_ge(id_in, 16)
            for j in range(NC):
                tok = slice(j * 512, (j + 1) * 512)
                if j >= 2:
                    pe.wait_ge(xnt_a, 2 * (j - 1))
                for i in range(4):
                    n = 4 * j + i
                    pe.wait_ge(xn_ready, n + 1)
                    for c in range(DC):
                        last = nc.tensor.transpose(PS[:, 2 * (j % 2) + c, i * P:(i + 1) * P],
                                                   XN[:, n, c * P:(c + 1) * P], ID[:])
                last.then_inc(tr_ready, 1)
                if j == 0:
                    pe.wait_ge(wq_in, 16)
                pe.wait_ge(xnt_a, 2 * (j + 1))
                if j >= 2:
                    pe.wait_ge(roped, j - 1)
                for c in range(DC):
                    last = nc.tensor.matmul(PS[:, 4 + j % 2, :], WQ[:, c, 0:P], XNT[:, c, tok],
                                            start=c == 0, stop=c == DC - 1)
                last.then_inc(k_ready, 1)
                if j == 1:
                    q_tile(0)
            for j in (1, 2):
                q_tile(j)
            for n in range(2 * NC):
                v_tile(n)
                if n == 4:
                    q_tile(3)

            def max_tile(b, u):
                i, c = divmod(u, 4)
                if not (isinstance(b, int) and b == 0 and u < 2):
                    pe.wait_ge(x_read, 16 * b + u - 1)
                nc.tensor.matmul(PS[:, 4 + u % 2, :],
                                 QC[0:KROWS, bass.ds(b, 1), i * P:(i + 1) * P].rearrange("p o n -> p (o n)"),
                                 KA[0:KROWS, bass.ds(kv_of(b) * L + c * 512, 512)],
                                 start=True, stop=True).then_inc(x_ready, 1)

            def max_transposes(b):
                pe.wait_ge(nm_d, 5 * b + 5)
                for i in range(4):
                    last = nc.tensor.transpose(MT[MROW:MROW + 4, i * P:(i + 1) * P], MP[:, i, :], IDB[:])
                last.then_inc(mt_ready, 1)

            def scores(b, s):
                for k in range(2):
                    last = nc.tensor.matmul(SCO[:, 2 * (s % 2) + k, :],
                                            KA[0:QROWS, bass.ds(kv_of(b) * L + (2 * s + k) * P, P)],
                                            QC[0:QROWS, bass.ds(b, 1), :].rearrange("p o n -> p (o n)"),
                                            start=True, stop=True)
                last.then_inc(s_ready, 1)

            def product(b, s, k):
                for i in range(4):
                    col = k * 512 + i * P
                    for w, p in enumerate((PHI, PR)):
                        last = nc.tensor.matmul(
                            ACC[:, i, :], p[:, s % 4, col:col + P],
                            VP[:, 2 * s + k, bass.ds(kv_of(b), 1), 0:ACCW].rearrange("p o e -> p (o e)"),
                            start=(s == 0 and k == 0 and i % 2 == 0 and w == 0),
                            stop=(s == STEPS - 1 and k == 1 and w == 1), skip_group_check=True)
                return last

            def tile(b, s, n, ahead):
                d, u = max_tiles(s)[n]
                if d <= ahead:
                    max_tile(b + d, u)

            def pe_block(b, first=False, ahead=2):
                for s in range(STEPS):
                    t = 8 * b + s
                    if s < STEPS - 2 or ahead >= 1:
                        pe.wait_ge(e_done, t + 1)
                        if s < STEPS - 2:
                            scores(b, s + 2)
                        else:
                            if s == STEPS - 2:
                                pe.wait_ge(m_rows, b + 2)
                            scores(b + 1, s - (STEPS - 2))
                    if s != 5:
                        tile(b, s, 0, ahead)
                    if s == 1 and ahead == 1:
                        pe.wait_ge(ones_set, 1)
                        pe.wait_ge(wabs, 3)
                        pe.wait_ge(x_read, 16 * NB)
                        nc.tensor.matmul(PS[:, 4, 256:259], ONES[:], WS[:, 0:3], start=True, stop=True).then_inc(wsum, 1)
                    if s == 4 and ahead == 1:
                        pe.wait_ge(wgam, 1)
                    if s == 0 and not first:
                        pe.wait_ge(evac, b)
                    pe.wait_ge(r_pool, t + 1)
                    product(b, s, 0)
                    if s == 5:
                        if ahead >= 2:
                            pe.wait_ge(m_rows, b + 2)
                        tile(b, s, 0, ahead)
                    tile(b, s, 1, ahead)
                    pe.wait_ge(r_dve, t + 1)
                    product(b, s, 1).then_inc(pv_done, 1)
                    if s == 4 and ahead >= 1:
                        if ahead >= 2:
                            pe.wait_ge(x_read, 16 * (b + 2) + max_tiles(4)[0][1] + 1)
                        max_transposes(b + 1)

            pe.wait_ge(k_in, 16 * len(TERMS))
            pe.wait_ge(roped, NC)
            pe.wait_ge(q_in[0], 16 * len(TERMS))
            pe.wait_ge(k_ones, 1)
            pe.wait_ge(idb_set, 2)
            pe.wait_ge(cst_set, 2)
            for u in range(16):
                max_tile(0, u)
            pe.wait_ge(x_read, 16)
            max_transposes(0)
            pe.wait_ge(m_rows, 1)
            pe.wait_ge(roped, NR)
            pe.wait_ge(q_in[1], 16 * len(TERMS))
            for u in range(AHEAD):
                max_tile(1, u)
                if u in (0, 6):
                    scores(0, u // 6)
            pe.wait_ge(vp_ready, 2)
            pe.wait_ge(v_sb, 2 * NC)
            pe.wait_ge(q_in[2], 16 * len(TERMS))
            pe_block(0, first=True)
            pe.wait_ge(q_in[3], 16 * len(TERMS))
            pe.wait_ge(q_in[4], 16 * len(TERMS))
            with pe.Fori(1, NB - 3, 2) as b:
                pe_block(b)
                pe_block(b + 1)
            pe_block(NB - 3)
            pe_block(NB - 2, ahead=1)
            pe_block(NB - 1, ahead=0)

            def turn(m):
                if m >= 1:
                    pe.wait_ge(ct_a, 2 * m)
                    pe.wait_ge(ct_d, 2 * m)
                pe.wait_ge(ctx_lo, (NH - 1) * NC + m // 2 + 1)
                for h in range(NH):
                    hp, c = h % 2, h // 2
                    for w in range(2):
                        last = nc.tensor.transpose(
                            PS[:, 2 * hp + w, c * P // 2:(c + 1) * P // 2].bitcast(fp16),
                            QF[:, h * NC + m // 2, w, 2 * (m % 2):2 * (m % 2) + 2, :].rearrange("p i e -> p (i e)"),
                            IDH[:])
                last.then_inc(ct_ready, 1)

            def project(n):
                pe.wait_ge((ct_d, ct_a)[n % 2], 2 * (n // 2 + 1))
                if n >= 2:
                    pe.wait_ge(y_read, n - 1)
                for c in range(OC):
                    for k, (w, v) in enumerate(((0, 0), (0, 1), (1, 0))):
                        last = nc.tensor.matmul(PS[:, 4 + n % 2, 0:D], CT[:, n // 2 % 2, n % 2, w, c, :],
                                                WO[:, v, c, :], start=(c == 0 and k == 0),
                                                stop=(c == OC - 1 and k == 2))
                last.then_inc(y_ready, 1)

            def second_turn(j):
                if j >= 1:
                    pe.wait_ge(t2_lo, 2 * j)
                for c in range(DC):
                    for i in range(4):
                        pe.wait_ge(x2_ready, 4 * j + i + 1)
                        last = nc.tensor.transpose(PS[:, 6 + c, i * P:(i + 1) * P],
                                                   X2[:, 4 * j + i, c * P:(c + 1) * P], ID[:])
                    last.then_inc(t2_ready, 1)

            pe.wait_ge(e_done, 8 * NB)
            turn(0)
            pe.wait_ge(wo_lo, 2)
            for m in range(NT // 2):
                if 0 < m < NT // 2 - 1:
                    turn(m + 1)
                project(2 * m)
                if m == 0:
                    turn(1)
                if m % 2 == 0 and m >= 2:
                    second_turn(m // 2 - 1)
                project(2 * m + 1)

            def up(i):
                j, f = divmod(i, len(FCH))
                h0, rows = FCH[f]
                tok = slice(j * 512, (j + 1) * 512)
                if i >= 3:
                    pe.wait_ge(hid_d, i - 2)
                for w, wq in enumerate((W1Q, W2Q)):
                    for c in range(DC):
                        for k, part in enumerate((T2H, T2L)):
                            last = nc.tensor.matmul(PS[0:rows, 2 * (i % 3) + w, :], wq[:, c, h0:h0 + rows],
                                                    part[:, c, tok], start=(c == 0 and k == 0),
                                                    stop=(c == DC - 1 and k == 1))
                last.then_inc(g_ready, 1)

            def down(j):
                pe.wait_ge(hl_d, (j + 1) * len(FCH))
                for i in range(4):
                    n = 4 * j + i
                    if n >= 2:
                        pe.wait_ge(o_sb, n - 1)
                    for f, (_, rows) in enumerate(FCH):
                        for k in range(2):
                            last = nc.tensor.matmul(PS[:, 6 + n % 2, 0:D], HP[0:rows, j % 2, k, f, i * P:(i + 1) * P],
                                                    W3Q[0:rows, f, :], start=(f == 0 and k == 0),
                                                    stop=(f == len(FCH) - 1 and k == 1))
                    last.then_inc(o_ready, 1)

            pe.wait_ge(w_tern, 3)
            for j in range(NC):
                pe.wait_ge(t2_lo, 2 * (j + 1))
                for f in range(len(FCH)):
                    if j == 0 and f == 2:
                        pe.wait_ge(y_read, NT)
                    up(j * len(FCH) + f)
                    if j == 0 and f == 2:
                        second_turn(NC - 1)
                if j == 1:
                    pe.wait_ge(t2_lo, 2 * NC)
                if j >= 1:
                    down(j - 1)
            down(NC - 1)


def kernel(**inputs):
    import concourse.bacc as bacc
    from concourse.bass_utils import run_bass_kernel_spmd

    def arr(name):
        return np.ascontiguousarray(inputs["L0_" + name])

    w = arr("attn_W_attn")
    qd, kd = NH * DK, NKV * DK
    qcols = np.arange(qd).reshape(NH, 2, HF)
    kcols = qd + np.arange(kd).reshape(NKV, 2, HF)
    order = np.concatenate([kcols.ravel(), kcols[:, ::-1].ravel(), qcols[:, 0].ravel(), qcols[:, 1].ravel(),
                            np.arange(qd + kd, w.shape[1])])
    inv = (np.float32(1.0) / np.float32(10000.0) ** (np.arange(0, DK, 2, dtype=np.float32) / np.float32(DK)))
    ang = inv.astype(np.float32)[:, None] * np.arange(L, dtype=np.float32)[None, :]
    half = np.float32(DK ** -0.25)
    arrays = {
        "x": arr("attn_x").reshape(L, D),
        "w_qkv": np.ascontiguousarray(w[:, order]),
        "w_out": arr("attn_W_out"),
        "b_out": arr("attn_b_out").reshape(1, D),
        "w1t": np.ascontiguousarray(arr("ffn_w1").T),
        "w2t": np.ascontiguousarray(arr("ffn_w2").T),
        "w3t": np.ascontiguousarray(arr("ffn_w3").T),
        "cos_t": np.tile(np.cos(ang) * half, (P // HF, 1)),
        "sin_t": np.tile(np.sin(ang) * half, (P // HF, 1)),
        "ksin_t": np.tile(np.concatenate([np.sin(ang) * -half, np.sin(ang) * half]), (NKV, 1)),
        "ident": np.eye(P, dtype=np.float32),
    }
    nc = bacc.Bacc("TRN2", target_bir_lowering=False, num_devices=1)
    args = [nc.dram_tensor(n + "_dram", a.shape, fp32, kind="ExternalInput").ap() for n, a in arrays.items()]
    out = nc.dram_tensor("out_dram", (L, D), fp32, kind="ExternalOutput").ap()
    layer(nc, *args, out)
    r = run_bass_kernel_spmd(nc, [{n + "_dram": a for n, a in arrays.items()}], core_ids=[0])
    return r.results[0]["out_dram"].reshape(1, L, D)
```
